# Optimizing a Trainium2 kernel written in Bass

```python
import numpy as np
import jax
import jax.numpy as jnp

def _softmax(x, axis=-1):
    return jax.nn.softmax(x, axis=axis)

def _gelu(x):
    return jax.nn.gelu(x, approximate=True)

def _silu(x):
    return jax.nn.silu(x)

def _sigmoid(x):
    return jax.nn.sigmoid(x)

def _layernorm(x, axis=-1, eps=1e-05):
    m = jnp.mean(x, axis=axis, keepdims=True)
    v = jnp.var(x, axis=axis, keepdims=True)
    return (x - m) / jnp.sqrt(v + eps)

def _scatter_add(tgt, idx, src, axis=0):
    return tgt.at[idx].add(src)

def _segment_sum(src, seg, n):
    return jax.ops.segment_sum(src, seg, n)
kernel_name = 'mk_seq_postln_d1_jaxref_r4_82b53e'

def setup_inputs(seed: int=0):
    np.random.seed(seed)
    _w = jnp.asarray

    def _L0_attn_setup():
        import jax, jax.numpy as jnp
        import numpy as np
        NUM_HEADS = 16
        ROPE_THETA = 10000.0

        def _rope_cos_sin(head_dim, seq_len, theta=ROPE_THETA):
            exps = -jnp.arange(0, head_dim, 2)[:head_dim // 2].astype(jnp.float32) / head_dim
            freqs = theta ** exps
            ang = jnp.arange(seq_len, dtype=jnp.float32)[:, None] * freqs[None, :]
            return (jnp.cos(ang), jnp.sin(ang))

        def _apply_rope(x, cos, sin):
            x2 = x.reshape(*x.shape[:-1], -1, 2)
            xr, xi = (x2[..., 0], x2[..., 1])
            c = cos[None, None]
            s = sin[None, None]
            outr = xr * c - xi * s
            outi = xr * s + xi * c
            return jnp.stack([outr, outi], axis=-1).reshape(x.shape)
        key = jax.random.key(seed)
        ks = jax.random.split(key, 9)
        B, S, D = (2, 512, 256)
        scale = 0.02
        x = jax.random.normal(ks[0], (B, S, D), jnp.float32)
        Wq = jax.random.normal(ks[1], (D, D), jnp.float32) * scale
        bq = jax.random.normal(ks[2], (D,), jnp.float32) * scale
        Wk = jax.random.normal(ks[3], (D, D), jnp.float32) * scale
        bk = jax.random.normal(ks[4], (D,), jnp.float32) * scale
        Wv = jax.random.normal(ks[5], (D, D), jnp.float32) * scale
        bv = jax.random.normal(ks[6], (D,), jnp.float32) * scale
        Wo = jax.random.normal(ks[7], (D, D), jnp.float32) * scale
        return {'x': x, 'Wq': Wq, 'bq': bq, 'Wk': Wk, 'bk': bk, 'Wv': Wv, 'bv': bv, 'Wo': Wo}
    _L0_attn_in = _L0_attn_setup()

    def _L0_ffn_setup():
        import jax, jax.numpy as jnp
        import numpy as np
        D_IN, D_HID = (256, 1024)

        def _ternary(key, shape):
            return jax.random.randint(key, shape, -1, 2).astype(jnp.float32)

        def _tlin(x, w, s):
            return jnp.einsum('bsi,oi->bso', x, w) * s
        key = jax.random.key(seed)
        ks = jax.random.split(key, 12)
        inv = lambda fan: 1.0 / np.sqrt(fan).astype(np.float32)
        return {'x': jax.random.normal(ks[0], (4, 512, D_IN), dtype=jnp.float32), 'w1_w': _ternary(ks[1], (D_HID, D_IN)), 'w1_s': jax.random.uniform(ks[2], (D_HID,), dtype=jnp.float32) * inv(D_IN), 'w2_w': _ternary(ks[3], (D_HID, D_IN)), 'w2_s': jax.random.uniform(ks[4], (D_HID,), dtype=jnp.float32) * inv(D_IN), 'h1_w': _ternary(ks[5], (D_HID, D_HID)), 'h1_s': jax.random.uniform(ks[6], (D_HID,), dtype=jnp.float32) * inv(D_HID), 'h2_w': _ternary(ks[7], (D_HID, D_HID)), 'h2_s': jax.random.uniform(ks[8], (D_HID,), dtype=jnp.float32) * inv(D_HID), 'w3_w': _ternary(ks[9], (D_IN, D_HID)), 'w3_s': jax.random.uniform(ks[10], (D_IN,), dtype=jnp.float32) * inv(D_HID)}
    _L0_ffn_in = _L0_ffn_setup()
    _d = {'L0_attn_x': _L0_attn_in['x'], 'L0_attn_Wq': _L0_attn_in['Wq'], 'L0_attn_bq': _L0_attn_in['bq'], 'L0_attn_Wk': _L0_attn_in['Wk'], 'L0_attn_bk': _L0_attn_in['bk'], 'L0_attn_Wv': _L0_attn_in['Wv'], 'L0_attn_bv': _L0_attn_in['bv'], 'L0_attn_Wo': _L0_attn_in['Wo'], 'L0_ffn_w1_w': _L0_ffn_in['w1_w'], 'L0_ffn_w1_s': _L0_ffn_in['w1_s'], 'L0_ffn_w2_w': _L0_ffn_in['w2_w'], 'L0_ffn_w2_s': _L0_ffn_in['w2_s'], 'L0_ffn_h1_w': _L0_ffn_in['h1_w'], 'L0_ffn_h1_s': _L0_ffn_in['h1_s'], 'L0_ffn_h2_w': _L0_ffn_in['h2_w'], 'L0_ffn_h2_s': _L0_ffn_in['h2_s'], 'L0_ffn_w3_w': _L0_ffn_in['w3_w'], 'L0_ffn_w3_s': _L0_ffn_in['w3_s']}
    _x0 = _d['L0_attn_x']
    _d['L0_attn_x'] = jax.random.normal(jax.random.fold_in(jax.random.key(seed), 1), (1, 4096, 256), dtype=_x0.dtype)
    del _x0
    return _d

def reference(L0_attn_x, L0_attn_Wq, L0_attn_bq, L0_attn_Wk, L0_attn_bk, L0_attn_Wv, L0_attn_bv, L0_attn_Wo, L0_ffn_w1_w, L0_ffn_w1_s, L0_ffn_w2_w, L0_ffn_w2_s, L0_ffn_h1_w, L0_ffn_h1_s, L0_ffn_h2_w, L0_ffn_h2_s, L0_ffn_w3_w, L0_ffn_w3_s):

    def _L0_attn_ref(x, Wq, bq, Wk, bk, Wv, bv, Wo):
        import jax, jax.numpy as jnp
        import numpy as np
        NUM_HEADS = 16
        ROPE_THETA = 10000.0

        def _rope_cos_sin(head_dim, seq_len, theta=ROPE_THETA):
            exps = -jnp.arange(0, head_dim, 2)[:head_dim // 2].astype(jnp.float32) / head_dim
            freqs = theta ** exps
            ang = jnp.arange(seq_len, dtype=jnp.float32)[:, None] * freqs[None, :]
            return (jnp.cos(ang), jnp.sin(ang))

        def _apply_rope(x, cos, sin):
            x2 = x.reshape(*x.shape[:-1], -1, 2)
            xr, xi = (x2[..., 0], x2[..., 1])
            c = cos[None, None]
            s = sin[None, None]
            outr = xr * c - xi * s
            outi = xr * s + xi * c
            return jnp.stack([outr, outi], axis=-1).reshape(x.shape)
        B, S, D = x.shape
        H = NUM_HEADS
        hd = D // H
        q = (x @ Wq.T + bq).reshape(B, S, H, hd).transpose(0, 2, 1, 3)
        k = (x @ Wk.T + bk).reshape(B, S, H, hd).transpose(0, 2, 1, 3)
        v = (x @ Wv.T + bv).reshape(B, S, H, hd).transpose(0, 2, 1, 3)
        cos, sin = _rope_cos_sin(hd, S)
        q = _apply_rope(q, cos, sin)
        k = _apply_rope(k, cos, sin)
        inv_scale = 1.0 / jnp.sqrt(jnp.asarray(D, jnp.float32))
        scores = jax.nn.softmax(jnp.einsum('bhqd,bhkd->bhqk', q, k) * inv_scale, axis=-1)
        out = jnp.einsum('bhqk,bhkd->bhqd', scores, v)
        out = out.transpose(0, 2, 1, 3).reshape(B, S, D)
        return out @ Wo.T

    def _L0_ffn_ref(x, w1_w, w1_s, w2_w, w2_s, h1_w, h1_s, h2_w, h2_s, w3_w, w3_s):
        import jax, jax.numpy as jnp
        import numpy as np
        D_IN, D_HID = (256, 1024)

        def _ternary(key, shape):
            return jax.random.randint(key, shape, -1, 2).astype(jnp.float32)

        def _tlin(x, w, s):
            return jnp.einsum('bsi,oi->bso', x, w) * s
        h = jax.nn.silu(_tlin(x, w1_w, w1_s)) * _tlin(x, w2_w, w2_s)
        h = jax.nn.gelu(_tlin(h, h1_w, h1_s), approximate=False)
        h = jax.nn.gelu(_tlin(h, h2_w, h2_s), approximate=False)
        return _tlin(h, w3_w, w3_s)
    x = L0_attn_x
    x = _layernorm(x + _L0_attn_ref(x, L0_attn_Wq, L0_attn_bq, L0_attn_Wk, L0_attn_bk, L0_attn_Wv, L0_attn_bv, L0_attn_Wo), axis=-1)
    x = _layernorm(x + _L0_ffn_ref(x, L0_ffn_w1_w, L0_ffn_w1_s, L0_ffn_w2_w, L0_ffn_w2_s, L0_ffn_h1_w, L0_ffn_h1_s, L0_ffn_h2_w, L0_ffn_h2_s, L0_ffn_w3_w, L0_ffn_w3_s), axis=-1)
    return x

_drawn_inputs = setup_inputs


def setup_inputs(seed=0):
    import zlib

    import numpy as np

    out = dict(_drawn_inputs(seed))
    spreads = {}
    factors = {'L0_attn_Wq': 8.0,
     'L0_attn_bq': 8.0,
     'L0_attn_Wk': 8.0,
     'L0_attn_bk': 8.0,
     'L0_attn_Wv': 8.0,
     'L0_attn_bv': 8.0,
     'L0_attn_Wo': 8.0,
     'L0_ffn_w1_w': 8.0,
     'L0_ffn_w1_s': 8.0,
     'L0_ffn_w2_w': 8.0,
     'L0_ffn_w2_s': 8.0,
     'L0_ffn_h1_w': 8.0,
     'L0_ffn_h1_s': 8.0,
     'L0_ffn_h2_w': 8.0,
     'L0_ffn_h2_s': 8.0,
     'L0_ffn_w3_w': 8.0,
     'L0_ffn_w3_s': 8.0}
    for name, (base, spread) in spreads.items():
        noise = np.random.default_rng([zlib.crc32(name.encode()), seed]).standard_normal(out[name].shape)
        drawn = base * np.exp(spread * noise) if base else spread * noise
        out[name] = jnp.asarray(drawn.astype(out[name].dtype))
    for name, factor in factors.items():
        out[name] = (out[name] * factor).astype(out[name].dtype)
    return out
```

```python
from contextlib import ExitStack

import concourse.bass as bass
from concourse import mybir

F32 = mybir.dt.float32
BF16 = mybir.dt.bfloat16
ALU = mybir.AluOpType
ACT = mybir.ActivationFunctionType
AX_X = mybir.AxisListType.X

P = 128
S, D, H = 4096, 256, 16
HD = D // H
HID = 1024
CH = 512
NCH = S // CH
TT = CH // P
NG = 4
HG = H // NG
KT = S // P
FT = D // P
HT = HID // P
EPS = 1e-5
INV_SCALE = 1.0 / float(D) ** 0.5

K_PART = [0, 1, 2, 0, 1, 0]
Q_PART = [0, 0, 0, 1, 1, 2]
NPROD = len(K_PART)
SHIFT_ROW = NPROD * HD
ROWS = SHIFT_ROW + 3




def project(nc, io, parts_dram, v_all):
    with ExitStack() as ctx:
        def sb(name, shape, dt=F32):
            return ctx.enter_context(nc.sbuf_tensor(name, shape, dt))

        def psum(name, shape):
            return ctx.enter_context(nc.psum_tensor(name, shape, F32))

        def sem(name):
            return ctx.enter_context(nc.semaphore(name))

        w_sb = sb("w_qk", [P, 4, FT, D])
        wv_sb = sb("w_v", [P, FT, D])
        b_sb = sb("b_qk", [P, 4, FT])
        bv_sb = sb("b_v", [P, D])
        xt = [sb(f"xt{p}", [P, FT, CH]) for p in range(2)]
        table = [sb(f"table{p}", [P, 2, CH]) for p in range(2)]
        turned = [sb(f"turned{b}", [P, 2, CH]) for b in range(2)]
        whole = [sb(f"whole{b}", [P, CH]) for b in range(2)]
        rest = [sb(f"rest{b}", [P, CH]) for b in range(2)]
        parts = [sb(f"parts{b}", [P, 3, CH], BF16) for b in range(2)]
        ps = [psum(f"ps_qk{b}", [P, 2, CH]) for b in range(2)]
        psv = [psum(f"ps_v{a}", [P, 2, D]) for a in range(2)]

        weights_in = sem("weights_in")
        x_in = [sem(f"x_in{p}") for p in range(2)]
        table_in = [sem(f"table_in{p}") for p in range(2)]
        qk_ready = sem("qk_ready")
        qk_free = sem("qk_free")
        v_ready = sem("v_ready")
        v_free = sem("v_free")
        turn = sem("turn")
        parts_free = [sem(f"parts_free{b}") for b in range(2)]
        ones_set = sem("ones_set")

        ITEMS = 2 * FT
        STEPS = 6
        WEIGHTS, TABLES = 10, 2 * P // HD

        block = ctx.enter_context(nc.Block())

        @block.sync
        def _(sp):
            for n, name in enumerate(["wqT", "wqrT", "wkT", "wkrT"]):
                sp.dma_start(w_sb[:, n], io[name].rearrange("(t p) o -> p t o", p=P)).then_inc(weights_in, 16)
            for n, name in enumerate(["bq", "bqr", "bk", "bkr"]):
                sp.dma_start(b_sb[:, n], io[name]).then_inc(weights_in, 16)
            sp.dma_start(wv_sb[:], io["wvT"].rearrange("(t p) o -> p t o", p=P)).then_inc(weights_in, 16)
            sp.dma_start(bv_sb[:], io["bv"].partition_broadcast(P)).then_inc(weights_in, 16)

            def load(p, c):
                cols = bass.ds(c * CH, CH)
                sp.dma_start(xt[p][:], io["xT"].rearrange("(t p) s -> p t s", p=P)[:, :, cols]).then_inc(x_in[p], 16)
                for n, name in enumerate(["cos", "sin"]):
                    for b in range(P // HD):
                        sp.dma_start(table[p][b * HD:(b + 1) * HD, n], io[name][:, cols]).then_inc(table_in[p], 16)

            def store(c):
                for m in range(ITEMS):
                    ft, t = m // 2, m % 2
                    sp.wait_ge(turn, (c * ITEMS + m + 1) * STEPS)
                    dst = parts_dram[t].rearrange("a f s -> f a s")[ft * P:(ft + 1) * P]
                    sp.dma_start(dst[:, :, bass.ds(c * CH, CH)], parts[m % 2][:]).then_inc(parts_free[m % 2], 16)

            load(0, 0)
            load(1, 1)
            with sp.Fori(0, NCH // 2 - 1) as cc:
                for p in range(2):
                    store(cc * 2 + p)
                    sp.wait_ge(v_ready, (cc * 2 + p + 1) * 2)
                    load(p, cc * 2 + p + 2)
            for p in range(2):
                store(NCH - 2 + p)
            for b in range(2):
                sp.wait_ge(parts_free[b], 16 + 16 * NCH * ITEMS // 2)

        @block.gpsimd
        def _(pool):
            pool.memset(v_all[:, :, :, :, HD:HD + 1], 1.0).then_inc(ones_set, 1)
            pool.wait_ge(ones_set, 1)

        @block.tensor
        def _(pe):
            pe.wait_ge(weights_in, 16 * WEIGHTS)
            with pe.Fori(0, NCH // 2) as cc:
                for p in range(2):
                    c = cc * 2 + p
                    pe.wait_ge(x_in[p], cc * 16 + 16)
                    for m in range(ITEMS):
                        ft, t = m // 2, m % 2
                        pe.wait_ge(qk_free, c * ITEMS + m + 1)
                        for r in range(2):
                            for i in range(FT):
                                last = pe.matmul(ps[m % 2][:, r], w_sb[:, 2 * t + r, i, ft * P:(ft + 1) * P],
                                                 xt[p][:, i], start=(i == 0), stop=(i == FT - 1))
                        last.then_inc(qk_ready, 1)
                    for a in range(2):
                        pe.wait_ge(v_free, c * 2 + a + 1)
                        for b in range(2):
                            tt = 2 * a + b
                            for i in range(FT):
                                last = pe.matmul(psv[a][:, b], xt[p][:, i, tt * P:(tt + 1) * P], wv_sb[:, i],
                                                 start=(i == 0), stop=(i == FT - 1))
                        last.then_inc(v_ready, 1)

        @block.vector
        def _(dve):
            dve.sem_inc(qk_free, 2)
            dve.sem_inc(v_free, 2)
            for b in range(2):
                dve.sem_inc(parts_free[b], 16)
            dve.wait_ge(weights_in, 16 * WEIGHTS)
            with dve.Fori(0, NCH // 2) as cc:
                for p in range(2):
                    c = cc * 2 + p
                    dve.wait_ge(table_in[p], cc * 16 * TABLES + 16 * TABLES)
                    for m in range(ITEMS):
                        ft, t, b = m // 2, m % 2, m % 2
                        base = (c * ITEMS + m) * STEPS
                        dve.wait_ge(qk_ready, c * ITEMS + m + 1)
                        dve.wait_ge(parts_free[b], (c * FT + ft) * 16 + 16)
                        dve.scalar_tensor_tensor(out=turned[b][:, 0], in0=ps[b][:, 0], scalar=b_sb[:, 2 * t, ft:ft + 1],
                                                 in1=table[p][:, 0], op0=ALU.add, op1=ALU.mult).then_inc(turn, 1)
                        dve.scalar_tensor_tensor(out=turned[b][:, 1], in0=ps[b][:, 1],
                                                 scalar=b_sb[:, 2 * t + 1, ft:ft + 1], in1=table[p][:, 1],
                                                 op0=ALU.add, op1=ALU.mult).then_inc(turn, 1)
                        dve.wait_ge(turn, base + 2)
                        dve.tensor_tensor(whole[b][:], turned[b][:, 0], turned[b][:, 1], ALU.add).then_inc(qk_free, 1)
                        dve.wait_ge(qk_free, c * ITEMS + m + 3)
                        dve.tensor_copy(parts[b][:, 0], whole[b][:]).then_inc(turn, 1)
                        dve.wait_ge(turn, base + 3)
                        dve.tensor_tensor(rest[b][:], whole[b][:], parts[b][:, 0], ALU.subtract).then_inc(turn, 1)
                        dve.wait_ge(turn, base + 4)
                        dve.tensor_copy(parts[b][:, 1], rest[b][:]).then_inc(turn, 1)
                        dve.wait_ge(turn, base + 5)
                        dve.tensor_tensor(parts[b][:, 2], rest[b][:], parts[b][:, 1], ALU.subtract).then_inc(turn, 1)
                    for a in range(2):
                        dve.wait_ge(v_ready, c * 2 + a + 1)
                        for b in range(2):
                            dst = v_all[:, :, bass.ds(c * TT + 2 * a + b, 1), :, 0:HD]
                            last = dve.tensor_tensor(dst.rearrange("p g a j d -> p (g a) j d"),
                                                     psv[a][:, b].rearrange("p (g j d) -> p g j d", g=NG, j=HG),
                                                     bv_sb[:].rearrange("p (g j d) -> p g j d", g=NG, j=HG), ALU.add)
                        last.then_inc(v_free, 1)
            dve.wait_ge(v_free, 2 + 2 * NCH)


def attend(nc, io, parts_dram, shift_dram, heads_dram, v_all):
    with ExitStack() as ctx:
        def sb(name, shape, dt=F32):
            return ctx.enter_context(nc.sbuf_tensor(name, shape, dt))

        def psum(name, shape):
            return ctx.enter_context(nc.psum_tensor(name, shape, F32))

        def sem(name):
            return ctx.enter_context(nc.semaphore(name))

        k_all = sb("k_all", [ROWS, NG, HG, S], BF16)
        q_sb = [sb(f"q_sb{p}", [ROWS, HG, CH], BF16) for p in range(2)]
        RING = 8
        probs = [sb(f"probs{r}", [P, 2, CH]) for r in range(RING)]
        mixed = [sb(f"mixed{p}", [P, CH]) for p in range(2)]
        scores = [psum(f"scores{b}", [P, 2, CH]) for b in range(2)]
        sums = [psum(f"sums{p}", [P, CH]) for p in range(2)]
        turned_max = psum("turned_max", [P, P])

        ident = probs[0][:, 0, 0:P]
        chunk_max = [probs[1][:, p, 0:HG * TT * 4] for p in range(2)]
        top = [probs[2][:, p, 0:HG * TT] for p in range(2)]
        top_rest = [probs[3][0:HG * TT, p, 0:P] for p in range(2)]
        top_parts = [probs[4][0:HG * TT, p, :].bitcast(BF16)[:, 0:3 * P].rearrange("r (a s) -> r a s", a=3)
                     for p in range(2)]

        k_in = [sem(f"k_in{g}") for g in range(NG)]
        k_ones = sem("k_ones")
        ident_set = sem("ident_set")
        mq_in = [sem(f"mq_in{p}") for p in range(2)]
        max_scores = sem("max_scores")
        max_free = sem("max_free")
        max_step = sem("max_step")
        max_turned = sem("max_turned")
        shift_out = [sem(f"shift_out{p}") for p in range(2)]
        q_in = [sem(f"q_in{p}") for p in range(2)]
        scored = sem("scored")
        exps_done = sem("exps_done")
        probs_free = sem("probs_free")
        sums_free = sem("sums_free")
        norm_step = sem("norm_step")
        waited = sem("waited")
        mixed_free = [sem(f"mixed_free{p}") for p in range(2)]

        UNITS = NCH * NG
        MAXG = HG * TT * 4
        GROUPS = KT * 2
        QLOADS = NPROD

        def load_q(sp, p, c, g, done):
            for r in range(NPROD):
                src = parts_dram[0][Q_PART[r]].rearrange("(h d) s -> d h s", d=HD)[:, g * HG:(g + 1) * HG]
                sp.dma_start(q_sb[p][r * HD:(r + 1) * HD], src[:, :, bass.ds(c * CH, CH)]).then_inc(done, 16)

        block = ctx.enter_context(nc.Block())

        @block.sync
        def _(sp):
            for p in range(2):
                load_q(sp, p, 0, p, mq_in[p])
            for g in range(NG):
                for r in range(NPROD):
                    src = parts_dram[1][K_PART[r]].rearrange("(h d) s -> d h s", d=HD)[:, g * HG:(g + 1) * HG]
                    sp.dma_start(k_all[r * HD:(r + 1) * HD, g], src).then_inc(k_in[g], 16)

            def store_shift(c, g):
                p = g % 2
                sp.wait_ge(max_step, (c * NG + g + 1) * 5)
                for j in range(HG):
                    dst = shift_dram[g * HG + j].rearrange("a (c t s) -> t c a s", c=NCH, t=TT)
                    sp.dma_start(dst[:, bass.ds(c, 1)].rearrange("t c a s -> (t c) a s"),
                                 top_parts[p][j * TT:(j + 1) * TT]).then_inc(shift_out[p], 16)

            with sp.Fori(0, NCH - 1) as c:
                for g in range(NG):
                    store_shift(c, g)
                    load_q(sp, g % 2, c if g < 2 else c + 1, (g + 2) % NG, mq_in[g % 2])
            for g in range(NG):
                store_shift(NCH - 1, g)
                if g < 2:
                    load_q(sp, g % 2, NCH - 1, g + 2, mq_in[g % 2])
            for p in range(2):
                sp.wait_ge(shift_out[p], 16 * HG + 16 * HG * UNITS // 2)

            def load_unit(c, g):
                load_q(sp, g % 2, c, g, q_in[g % 2])
                src = shift_dram[g * HG:(g + 1) * HG].rearrange("h a s -> a h s")
                sp.dma_start(q_sb[g % 2][SHIFT_ROW:ROWS], src[:, :, bass.ds(c * CH, CH)]).then_inc(q_in[g % 2], 16)

            def store_unit(c, g):
                sp.wait_ge(sums_free, c * NG + g + 3)
                sp.dma_start(heads_dram[bass.ds(c, 1), :, g].rearrange("c p s -> (c p) s"), mixed[g % 2][:])\
                    .then_inc(mixed_free[g % 2], 16)

            for g in range(2):
                load_unit(0, g)
            with sp.Fori(0, NCH - 1) as c:
                for g in range(NG):
                    store_unit(c, g)
                    load_unit(c if g < 2 else c + 1, (g + 2) % NG)
            for g in range(NG):
                store_unit(NCH - 1, g)
                if g < 2:
                    load_unit(NCH - 1, g + 2)
            for p in range(2):
                sp.wait_ge(mixed_free[p], 16 + 16 * UNITS // 2)

        @block.gpsimd
        def _(pool):
            pool.memset(ident, 0.0).then_inc(ident_set, 1)
            pool.wait_ge(ident_set, 1)
            pool.affine_select(out=ident, in_=ident, compare_op=ALU.not_equal, fill=1.0, base=0,
                               pattern=[[-1, P]], channel_multiplier=1).then_inc(ident_set, 1)
            pool.wait_ge(ident_set, 2)
            for g in range(NG):
                pool.memset(k_all[SHIFT_ROW:ROWS, g], 1.0).then_inc(k_ones, 1)
                pool.wait_ge(k_ones, g + 1)

        @block.tensor
        def _(pe):
            pe.wait_ge(ident_set, 2)
            pe.wait_ge(k_ones, NG)
            for g in range(NG):
                pe.wait_ge(k_in[g], 16 * NPROD)

            with pe.Fori(0, NCH) as c:
                for g in range(NG):
                    p = g % 2
                    pe.wait_ge(mq_in[p], (c * 2 + g // 2) * (16 * NPROD) + 16 * NPROD)
                    for j in range(HG):
                        for t in range(TT):
                            for b in range(4):
                                n = (j * TT + t) * 4 + b
                                pe.wait_ge(max_free, (c * NG + g) * MAXG + n + 1)
                                for h in range(2):
                                    keys = slice((2 * b + h) * CH, (2 * b + h + 1) * CH)
                                    last = pe.matmul(scores[b % 2][:, h], q_sb[p][0:SHIFT_ROW, j, t * P:(t + 1) * P],
                                                     k_all[0:SHIFT_ROW, g, j, keys], start=True, stop=True)
                                last.then_inc(max_scores, 1)
                    pe.wait_ge(max_step, (c * NG + g) * 5 + 1)
                    pe.transpose(turned_max[0:HG * TT, :], top[p], ident).then_inc(max_turned, 1)

            def unit(c, g):
                p, u = g % 2, c * NG + g
                pe.wait_ge(q_in[p], (c * 2 + g // 2) * (16 * (NPROD + 1)) + 16 * (NPROD + 1))

                def sum_over(kt):
                    if kt == 0:
                        pe.wait_ge(sums_free, u + 1)
                    pe.wait_ge(exps_done, u * GROUPS + 2 * kt + 2 + 2)
                    for j in range(HG):
                        last = pe.matmul(sums[p][32 * j:32 * j + HD + 1, :], v_all[:, g, kt, j],
                                         probs[(2 * kt + j // 2) % RING][:, j % 2], start=(kt == 0), stop=(kt == KT - 1))
                    last.then_inc(probs_free, 1)

                for n in range(GROUPS):
                    kt = n // 2
                    pe.wait_ge(exps_done, u * GROUPS + n + 1)
                    for h in range(2):
                        j = 2 * (n % 2) + h
                        last = pe.matmul(scores[n % 2][:, h], k_all[:, g, j, kt * P:(kt + 1) * P], q_sb[p][:, j],
                                         start=True, stop=True)
                    last.then_inc(scored, 1)
                    if n >= 4 and n % 2 == 1:
                        sum_over(kt - 2)
                sum_over(KT - 2)
                sum_over(KT - 1)

            with pe.Fori(0, NCH) as c:
                for g in range(NG):
                    unit(c, g)

        @block.scalar
        def _(act):
            act.sem_inc(exps_done, 2)
            act.sem_inc(probs_free, RING // 2)
            with act.Fori(0, NCH) as c:
                for g in range(NG):
                    for n in range(GROUPS):
                        act.wait_ge(scored, (c * NG + g) * GROUPS + n + 1)
                        if n % 2 == 0:
                            act.wait_ge(probs_free, (c * NG + g) * KT + n // 2 + 1)
                        act.activation(probs[n % RING][:], scores[n % 2][:], ACT.Exp, scale=INV_SCALE)\
                            .then_inc(exps_done, 1)

        @block.vector
        def _(dve):
            dve.sem_inc(max_free, 2)
            for p in range(2):
                dve.sem_inc(shift_out[p], 16 * HG)
                dve.sem_inc(mixed_free[p], 16)
                dve.memset(sums[p][:], 0.0).then_inc(sums_free, 1)
            with dve.Fori(0, NCH) as c:
                for g in range(NG):
                    p, u = g % 2, c * NG + g
                    for n in range(MAXG):
                        dve.wait_ge(max_scores, u * MAXG + n + 1)
                        dve.reduce_max(chunk_max[p][:, n:n + 1], scores[n % 2][:], mybir.AxisListType.XY)\
                            .then_inc(max_free, 1)
                    dve.wait_ge(max_free, (u + 1) * MAXG + 2)
                    dve.reduce_max(top[p], chunk_max[p].rearrange("q (r b) -> q r b", b=4), AX_X).then_inc(max_step, 1)
                    dve.wait_ge(max_turned, u + 1)
                    dve.wait_ge(shift_out[p], (c * 2 + g // 2) * (16 * HG) + 16 * HG)
                    turned = turned_max[0:HG * TT, :]
                    dve.tensor_scalar(top_parts[p][:, 0], turned, -1.0, None, ALU.mult).then_inc(max_step, 1)
                    dve.wait_ge(max_step, u * 5 + 2)
                    dve.scalar_tensor_tensor(out=top_rest[p], in0=turned, scalar=-1.0, in1=top_parts[p][:, 0],
                                             op0=ALU.mult, op1=ALU.subtract).then_inc(max_step, 1)
                    dve.wait_ge(max_step, u * 5 + 3)
                    dve.tensor_copy(top_parts[p][:, 1], top_rest[p]).then_inc(max_step, 1)
                    dve.wait_ge(max_step, u * 5 + 4)
                    dve.tensor_tensor(top_parts[p][:, 2], top_rest[p], top_parts[p][:, 1], ALU.subtract)\
                        .then_inc(max_step, 1)

            with dve.Fori(0, NCH) as c:
                for g in range(NG):
                    p, u = g % 2, c * NG + g
                    dve.wait_ge(probs_free, (u + 1) * KT + RING // 2)
                    dve.wait_ge(mixed_free[p], (c * 2 + g // 2) * 16 + 16)
                    dve.sem_inc(waited, 1)
                    dve.stream_shuffle(mixed[p][:], sums[p][:], [HD] * 32).then_inc(norm_step, 1)
                    dve.wait_ge(norm_step, u * 2 + 1)
                    dve.reciprocal(mixed[p][:], mixed[p][:]).then_inc(norm_step, 1)
                    dve.wait_ge(norm_step, u * 2 + 2)
                    dve.tensor_tensor(mixed[p][:], sums[p][:], mixed[p][:], ALU.mult).then_inc(sums_free, 1)


def feed_forward(nc, io, heads_dram, out):
    with ExitStack() as ctx:
        def sb(name, shape, dt=F32):
            return ctx.enter_context(nc.sbuf_tensor(name, shape, dt))

        def psum(name, shape):
            return ctx.enter_context(nc.psum_tensor(name, shape, F32))

        def sem(name):
            return ctx.enter_context(nc.semaphore(name))

        wo = sb("wo", [P, NG, D])
        w1, w2 = sb("w1", [P, FT, HID]), sb("w2", [P, FT, HID])
        h1, h2 = sb("h1", [P, HT, HID]), sb("h2", [P, HT, HID])
        w3 = sb("w3", [P, HT, D])
        scale = sb("scale", [P, 4, HT])
        scale3 = sb("scale3", [P, D])
        ident = sb("ident_ff", [P, P])
        heads = [sb(f"heads{p}", [P, NG, CH]) for p in range(2)]
        x_sb = [sb(f"x_sb{p}", [P, TT, D]) for p in range(2)]
        x1 = [sb(f"x1_{p}", [P, TT, D]) for p in range(2)]
        x1t = [sb(f"x1t{p}", [P, FT, CH]) for p in range(2)]
        hid_a, hid_b = sb("hid_a", [P, HT, CH]), sb("hid_b", [P, HT, CH])
        gate = [sb(f"gate{b}", [P, CH]) for b in range(4)]
        fin = [sb(f"fin{p}", [P, TT, D]) for p in range(2)]
        stats = [sb(f"stats{i}", [P, TT, 6]) for i in range(2)]
        moments = [sb(f"moments{i}", [P, TT, 2]) for i in range(2)]
        spread = [sb(f"spread{i}", [P, TT]) for i in range(2)]
        root = [sb(f"root{i}", [P, TT]) for i in range(2)]
        inverse = [sb(f"inverse{i}", [P, TT]) for i in range(2)]
        acc = [psum(f"acc{b}", [P, CH]) for b in range(4)]
        tok = [psum(f"tok{b}", [P, 2, D]) for b in range(2)]
        flip = [psum(f"flip{b}", [P, CH]) for b in range(2)]

        weights_in = sem("ff_weights_in")
        heads_in = [sem(f"heads_in{p}") for p in range(2)]
        x_ff_in = [sem(f"x_ff_in{p}") for p in range(2)]
        wo_zero = sem("wo_zero")
        ident_set = sem("ident_ff_set")
        acc_ready = sem("acc_ready")
        gated = sem("gated")
        hid_ready = sem("hid_ready")
        tok_ready = sem("tok_ready")
        norm1 = sem("norm1")
        norm2 = sem("norm2")
        root_done = sem("root_done")
        flip_ready = sem("flip_ready")
        x1t_ready = sem("x1t_ready")
        waited = sem("ff_waited")
        fin_free = [sem(f"fin_free{p}") for p in range(2)]

        ACCS = 4 * HT
        HIDS = 3 * HT
        NORM1 = 4 * TT + 2
        NORM2 = 5 * TT + 2
        WEIGHTS = HG + 4 + 5 + 1

        block = ctx.enter_context(nc.Block())

        @block.sync
        def _(sp):
            def load(c, p):
                sp.dma_start(heads[p][:], heads_dram[bass.ds(c, 1)].rearrange("c p g s -> (c p) g s"))\
                    .then_inc(heads_in[p], 16)
                sp.dma_start(x_sb[p][:], io["x"].rearrange("(c t p) d -> c p t d", t=TT, p=P)[bass.ds(c, 1)]
                             .rearrange("c p t d -> (c p) t d")).then_inc(x_ff_in[p], 16)

            def store(c, p):
                sp.wait_ge(norm2, (c + 2) * NORM2)
                sp.dma_start(out.rearrange("(c t p) d -> c p t d", t=TT, p=P)[bass.ds(c, 1)]
                             .rearrange("c p t d -> (c p) t d"), fin[p][:]).then_inc(fin_free[p], 16)

            sp.wait_ge(wo_zero, 1)
            for j in range(HG):
                sp.dma_start(wo[32 * j:32 * j + HD], io["woT"].rearrange("(g j d) o -> j d g o", g=NG, j=HG)[j])\
                    .then_inc(weights_in, 16)
            load(0, 0)
            for n, name in enumerate(["w1_s", "w2_s", "h1_s", "h2_s"]):
                sp.dma_start(scale[:, n], io[name]).then_inc(weights_in, 16)
            for dst, name in [(w1, "w1T"), (w2, "w2T"), (h1, "h1T"), (h2, "h2T"), (w3, "w3T")]:
                sp.dma_start(dst[:], io[name].rearrange("(t p) o -> p t o", p=P)).then_inc(weights_in, 16)
            sp.dma_start(scale3[:], io["w3_s"].partition_broadcast(P)).then_inc(weights_in, 16)
            load(1, 1)
            with sp.Fori(0, NCH // 2 - 1) as cc:
                for p in range(2):
                    c = cc * 2 + p
                    store(c, p)
                    load(c + 2, p)
            for p in range(2):
                store(NCH - 2 + p, p)
            for p in range(2):
                sp.wait_ge(fin_free[p], 16 + 16 * NCH // 2)

        @block.gpsimd
        def _(pool):
            pool.memset(wo[:], 0.0).then_inc(wo_zero, 1)
            pool.wait_ge(wo_zero, 1)
            pool.memset(ident[:], 0.0).then_inc(ident_set, 1)
            pool.wait_ge(ident_set, 1)
            pool.affine_select(out=ident[:], in_=ident[:], compare_op=ALU.not_equal, fill=1.0, base=0,
                               pattern=[[-1, P]], channel_multiplier=1).then_inc(ident_set, 1)

        def front_turn(c):
            return 0 if isinstance(c, int) and c == 0 else c * 2 - 1

        def back_turn(c, last):
            return c * 2 + 1 if last else c * 2 + 2

        @block.tensor
        def _(pe):
            def front(c, half, p):
                pe.wait_ge(heads_in[p], half * 16 + 16)
                for t in range(TT):
                    if t % 2 == 0 and not (isinstance(c, int) and c == 0):
                        pe.wait_ge(norm2, (c - 1) * NORM2 + t + 2)
                    for g in range(NG):
                        last = pe.matmul(tok[t // 2][:, t % 2], heads[p][:, g, t * P:(t + 1) * P], wo[:, g],
                                         start=(g == 0), stop=(g == NG - 1))
                    if t % 2 == 1:
                        last.then_inc(tok_ready, 1)

            def front_flip(c, p):
                pe.wait_ge(norm1, (c + 1) * NORM1)
                for f in range(FT):
                    for t in range(TT):
                        last = pe.transpose(flip[f][:, t * P:(t + 1) * P], x1[p][:, t, f * P:(f + 1) * P], ident[:])
                    last.then_inc(flip_ready, 1)

            def acc_read(c, n):
                if n < 2 * HT and n % 2 == 0:
                    pe.wait_ge(gated, c * HT + n // 2 + 1)
                elif n < 2 * HT:
                    pe.wait_ge(hid_ready, c * HIDS + n // 2 + 1)
                else:
                    pe.wait_ge(hid_ready, c * HIDS + (n - HT) + 1)

            def gate_layer(c, p):
                pe.wait_ge(x1t_ready, (c + 1) * FT)
                for o in range(HT):
                    for w, wt in enumerate((w1, w2)):
                        n = 2 * o + w
                        if n >= 4:
                            acc_read(c, n - 4)
                        for i in range(FT):
                            last = pe.matmul(acc[n % 4][:], wt[:, i, o * P:(o + 1) * P], x1t[p][:, i],
                                             start=(i == 0), stop=(i == FT - 1))
                        last.then_inc(acc_ready, 1)

            def hidden_layer(c, layer):
                src, wt = ((hid_a, h1), (hid_b, h2))[layer]
                for o in range(HT):
                    n = (2 + layer) * HT + o
                    acc_read(c, n - 4)
                    for i in range(HT):
                        if o == 0:
                            pe.wait_ge(hid_ready, c * HIDS + layer * HT + i + 1)
                        last = pe.matmul(acc[n % 4][:], wt[:, i, o * P:(o + 1) * P], src[:, i],
                                         start=(i == 0), stop=(i == HT - 1))
                    last.then_inc(acc_ready, 1)

            def back(c, final):
                pe.wait_ge(hid_ready, (c + 1) * HIDS)
                for t in range(TT):
                    if t % 2 == 0 and final:
                        pe.wait_ge(norm2, c * NORM2 + t + 2)
                    for i in range(HT):
                        last = pe.matmul(tok[t // 2][:, t % 2], hid_a[:, i, t * P:(t + 1) * P], w3[:, i],
                                         start=(i == 0), stop=(i == HT - 1))
                    if t % 2 == 1:
                        last.then_inc(tok_ready, 1)

            def chunk(half, p, final=False):
                c = half * 2 + p
                gate_layer(c, p)
                if not final:
                    front(c + 1, half + p, 1 - p)
                hidden_layer(c, 0)
                if not final:
                    front_flip(c + 1, 1 - p)
                hidden_layer(c, 1)
                back(c, final)

            pe.wait_ge(ident_set, 2)
            pe.wait_ge(weights_in, 16 * WEIGHTS)
            front(0, 0, 0)
            front_flip(0, 0)
            with pe.Fori(0, NCH // 2 - 1) as half:
                for p in range(2):
                    chunk(half, p)
            chunk(NCH // 2 - 1, 0)
            chunk(NCH // 2 - 1, 1, final=True)

        @block.scalar
        def _(act):
            def front_root(c):
                act.wait_ge(norm1, c * NORM1 + 3 * TT + 1)
                act.activation(root[0][:], spread[0][:], ACT.Sqrt).then_inc(root_done, 1)

            def front_flip(c, p):
                for f in range(FT):
                    act.wait_ge(flip_ready, c * FT + f + 1)
                    act.activation(x1t[p][:, f], flip[f][:], ACT.Copy).then_inc(x1t_ready, 1)

            def gates(c):
                for o in range(HT):
                    act.wait_ge(acc_ready, c * ACCS + 2 * o + 1)
                    if o >= 4:
                        act.wait_ge(hid_ready, c * HIDS + o - 3)
                    act.activation(gate[o % 4][:], acc[(2 * o) % 4][:], ACT.Silu, scale=scale[:, 0, o:o + 1])\
                        .then_inc(gated, 1)

            def gelus(c, layer):
                dst = (hid_b, hid_a)[layer]
                for o in range(HT):
                    n = (2 + layer) * HT + o
                    act.wait_ge(acc_ready, c * ACCS + n + 1)
                    act.activation(dst[:, o], acc[n % 4][:], ACT.Gelu, scale=scale[:, 2 + layer, o:o + 1])\
                        .then_inc(hid_ready, 1)

            def back_root(c):
                act.wait_ge(norm2, (c + 1) * NORM2 + 4 * TT + 1)
                act.activation(root[1][:], spread[1][:], ACT.Sqrt).then_inc(root_done, 1)

            def chunk(half, p, final=False):
                c = half * 2 + p
                gates(c)
                if not final:
                    front_root(c + 1)
                gelus(c, 0)
                if not final:
                    front_flip(c + 1, 1 - p)
                gelus(c, 1)
                back_root(c)

            act.wait_ge(weights_in, 16 * WEIGHTS)
            front_root(0)
            front_flip(0, 0)
            with act.Fori(0, NCH // 2 - 1) as half:
                for p in range(2):
                    chunk(half, p)
            chunk(NCH // 2 - 1, 0)
            chunk(NCH // 2 - 1, 1, final=True)

        @block.vector
        def _(dve):
            def normalise(i, data, dst, done, base, turn):
                for t in range(TT):
                    dve.wait_ge(done, base - TT + t + 1)
                    dve.bn_stats(stats[i][:, t], data[:, t]).then_inc(done, 1)
                for t in range(TT):
                    dve.wait_ge(done, base + t + 1)
                    dve.sem_inc(waited, 1)
                    dve.bn_aggr(moments[i][:, t], stats[i][:, t]).then_inc(done, 1)
                dve.wait_ge(done, base + 2 * TT)
                dve.tensor_scalar(spread[i][:], moments[i][:, :, 1], EPS, None, ALU.add).then_inc(done, 1)
                dve.wait_ge(root_done, turn + 1)
                dve.reciprocal(inverse[i][:], root[i][:]).then_inc(done, 1)
                dve.wait_ge(done, base + 2 * TT + 2)
                for t in range(TT):
                    dve.tensor_scalar(dst[:, t], data[:, t], moments[i][:, t, 0:1], inverse[i][:, t:t + 1],
                                      ALU.subtract, ALU.mult).then_inc(done, 1)

            def front(c, half, p):
                turn = front_turn(c)
                dve.wait_ge(x_ff_in[p], half * 16 + 16)
                for t in range(TT):
                    if t % 2 == 0:
                        dve.wait_ge(tok_ready, turn * 2 + t // 2 + 1)
                    dve.tensor_tensor(x1[p][:, t], tok[t // 2][:, t % 2], x_sb[p][:, t], ALU.add).then_inc(norm1, 1)
                normalise(0, x1[p], x1[p], norm1, c * NORM1 + TT, turn)

            def gates(c):
                for o in range(HT):
                    dve.wait_ge(gated, c * HT + o + 1)
                    dve.wait_ge(acc_ready, c * ACCS + 2 * o + 2)
                    dve.scalar_tensor_tensor(out=hid_a[:, o], in0=acc[(2 * o + 1) % 4][:], scalar=scale[:, 1, o:o + 1],
                                             in1=gate[o % 4][:], op0=ALU.mult, op1=ALU.mult).then_inc(hid_ready, 1)

            def back(c, half, p, final):
                turn, base = back_turn(c, final), (c + 1) * NORM2
                dve.wait_ge(fin_free[p], half * 16 + 16)
                for t in range(TT):
                    if t % 2 == 0:
                        dve.wait_ge(tok_ready, turn * 2 + t // 2 + 1)
                    dve.tensor_tensor(fin[p][:, t], tok[t // 2][:, t % 2], scale3[:], ALU.mult).then_inc(norm2, 1)
                for t in range(TT):
                    dve.wait_ge(norm2, base + t + 1)
                    dve.tensor_tensor(fin[p][:, t], fin[p][:, t], x1[p][:, t], ALU.add).then_inc(norm2, 1)
                normalise(1, fin[p], fin[p], norm2, base + 2 * TT, turn)

            def chunk(half, p, final=False):
                c = half * 2 + p
                gates(c)
                if not final:
                    front(c + 1, half + p, 1 - p)
                back(c, half, p, final)

            dve.sem_inc(norm2, NORM2)
            for p in range(2):
                dve.sem_inc(fin_free[p], 16)
            dve.wait_ge(weights_in, 16 * WEIGHTS)
            front(0, 0, 0)
            with dve.Fori(0, NCH // 2 - 1) as half:
                for p in range(2):
                    chunk(half, p)
            chunk(NCH // 2 - 1, 0)
            chunk(NCH // 2 - 1, 1, final=True)


def build(nc, io, out):
    parts_dram = [nc.dram_tensor(f"{t}_parts", [3, D, S], BF16, kind="Internal").ap() for t in "qk"]
    shift_dram = nc.dram_tensor("shifts", [H, 3, S], BF16, kind="Internal").ap()
    heads_dram = nc.dram_tensor("heads", [NCH, P, NG, CH], F32, kind="Internal").ap()
    with nc.sbuf_tensor("v_all", [P, NG, KT, HG, HD + 1], F32) as v_all:
        project(nc, io, parts_dram, v_all)
        attend(nc, io, parts_dram, shift_dram, heads_dram, v_all)
    feed_forward(nc, io, heads_dram, out)


def kernel(**inputs):
    import numpy as np
    import concourse.bacc as bacc
    from concourse.bass_utils import run_bass_kernel_spmd

    a = {k.removeprefix("L0_"): np.asarray(v) for k, v in inputs.items()}
    pair = np.arange(D).reshape(D // 2, 2)[:, ::-1].reshape(D)

    def columns(v):
        return v.reshape(-1, P).T

    freqs = np.float32(10000.0) ** (-np.arange(0, HD, 2).astype(np.float32) / np.float32(HD))
    angle = np.arange(S, dtype=np.float32)[:, None] * freqs[None, :]
    cos, sin = np.cos(angle), np.sin(angle)
    cos_rows = np.stack([cos, cos], axis=-1).reshape(S, HD).T
    sin_rows = np.stack([-sin, sin], axis=-1).reshape(S, HD).T

    arrays = {
        "x": a["attn_x"][0], "xT": a["attn_x"][0].T,
        "wqT": a["attn_Wq"].T, "wqrT": a["attn_Wq"][pair].T, "wkT": a["attn_Wk"].T, "wkrT": a["attn_Wk"][pair].T,
        "wvT": a["attn_Wv"].T, "woT": a["attn_Wo"].T,
        "bq": columns(a["attn_bq"]), "bqr": columns(a["attn_bq"][pair]),
        "bk": columns(a["attn_bk"]), "bkr": columns(a["attn_bk"][pair]), "bv": a["attn_bv"],
        "cos": cos_rows, "sin": sin_rows,
        "w1T": a["ffn_w1_w"].T, "w2T": a["ffn_w2_w"].T, "h1T": a["ffn_h1_w"].T, "h2T": a["ffn_h2_w"].T,
        "w3T": a["ffn_w3_w"].T,
        "w1_s": columns(a["ffn_w1_s"]), "w2_s": columns(a["ffn_w2_s"]),
        "h1_s": columns(a["ffn_h1_s"]), "h2_s": columns(a["ffn_h2_s"]), "w3_s": a["ffn_w3_s"],
    }
    arrays = {k: np.ascontiguousarray(v) for k, v in arrays.items()}
    nc = bacc.Bacc("TRN2", target_bir_lowering=False, num_devices=1)
    io = {k: nc.dram_tensor(f"in_{k}", v.shape, mybir.dt.from_np(v.dtype), kind="ExternalInput").ap()
          for k, v in arrays.items()}
    out = nc.dram_tensor("out_0", [S, D], F32, kind="ExternalOutput").ap()
    build(nc, io, out)
    r = run_bass_kernel_spmd(nc, [{f"in_{k}": v for k, v in arrays.items()}], core_ids=[0])
    return r.results[0]["out_0"].reshape(1, S, D)
```

```python
from contextlib import ExitStack

import concourse.bass as bass
from concourse import mybir

F32 = mybir.dt.float32
BF16 = mybir.dt.bfloat16
ALU = mybir.AluOpType
ACT = mybir.ActivationFunctionType
AX_X = mybir.AxisListType.X

P = 128
S, D, H = 4096, 256, 16
HD = D // H
HID = 1024
CH = 512
NCH = S // CH
TT = CH // P
NG = 4
HG = H // NG
KT = S // P
FT = D // P
HT = HID // P
EPS = 1e-5
INV_SCALE = 1.0 / float(D) ** 0.5

K_PART = [0, 1, 2, 0, 1, 0]
Q_PART = [0, 0, 0, 1, 1, 2]
NPROD = len(K_PART)
SHIFT_ROW = NPROD * HD
ROWS = SHIFT_ROW + 3




def project(nc, io, parts_dram, v_all):
    with ExitStack() as ctx:
        def sb(name, shape, dt=F32):
            return ctx.enter_context(nc.sbuf_tensor(name, shape, dt))

        def psum(name, shape):
            return ctx.enter_context(nc.psum_tensor(name, shape, F32))

        def sem(name):
            return ctx.enter_context(nc.semaphore(name))

        w_sb = sb("w_qk", [P, 4, FT, D])
        wv_sb = sb("w_v", [P, FT, D])
        b_sb = sb("b_qk", [P, 4, FT])
        bv_sb = sb("b_v", [P, D])
        xt = [sb(f"xt{p}", [P, FT, CH]) for p in range(2)]
        table = [sb(f"table{p}", [P, 2, CH]) for p in range(2)]
        turned = [sb(f"turned{b}", [P, 2, CH]) for b in range(2)]
        whole = [sb(f"whole{b}", [P, CH]) for b in range(2)]
        rest = [sb(f"rest{b}", [P, CH]) for b in range(2)]
        parts = [sb(f"parts{b}", [P, 3, CH], BF16) for b in range(2)]
        ps = [psum(f"ps_qk{b}", [P, 2, CH]) for b in range(2)]
        psv = [psum(f"ps_v{a}", [P, 2, D]) for a in range(2)]

        weights_in = sem("weights_in")
        x_in = [sem(f"x_in{p}") for p in range(2)]
        table_in = [sem(f"table_in{p}") for p in range(2)]
        qk_ready = sem("qk_ready")
        qk_free = sem("qk_free")
        v_ready = sem("v_ready")
        v_free = sem("v_free")
        turn = sem("turn")
        parts_free = [sem(f"parts_free{b}") for b in range(2)]
        ones_set = sem("ones_set")

        ITEMS = 2 * FT
        STEPS = 6
        WEIGHTS, TABLES = 10, 2 * P // HD

        block = ctx.enter_context(nc.Block())

        @block.sync
        def _(sp):
            for n, name in enumerate(["wqT", "wqrT", "wkT", "wkrT"]):
                sp.dma_start(w_sb[:, n], io[name].rearrange("(t p) o -> p t o", p=P)).then_inc(weights_in, 16)
            for n, name in enumerate(["bq", "bqr", "bk", "bkr"]):
                sp.dma_start(b_sb[:, n], io[name]).then_inc(weights_in, 16)
            sp.dma_start(wv_sb[:], io["wvT"].rearrange("(t p) o -> p t o", p=P)).then_inc(weights_in, 16)
            sp.dma_start(bv_sb[:], io["bv"].partition_broadcast(P)).then_inc(weights_in, 16)

            def load(p, c):
                cols = bass.ds(c * CH, CH)
                sp.dma_start(xt[p][:], io["xT"].rearrange("(t p) s -> p t s", p=P)[:, :, cols]).then_inc(x_in[p], 16)
                for n, name in enumerate(["cos", "sin"]):
                    for b in range(P // HD):
                        sp.dma_start(table[p][b * HD:(b + 1) * HD, n], io[name][:, cols]).then_inc(table_in[p], 16)

            def store(c):
                for m in range(ITEMS):
                    ft, t = m // 2, m % 2
                    sp.wait_ge(turn, (c * ITEMS + m + 1) * STEPS)
                    dst = parts_dram[t].rearrange("a f s -> f a s")[ft * P:(ft + 1) * P]
                    sp.dma_start(dst[:, :, bass.ds(c * CH, CH)], parts[m % 2][:]).then_inc(parts_free[m % 2], 16)

            load(0, 0)
            load(1, 1)
            with sp.Fori(0, NCH // 2 - 1) as cc:
                for p in range(2):
                    store(cc * 2 + p)
                    sp.wait_ge(v_ready, (cc * 2 + p + 1) * 2)
                    load(p, cc * 2 + p + 2)
            for p in range(2):
                store(NCH - 2 + p)
            for b in range(2):
                sp.wait_ge(parts_free[b], 16 + 16 * NCH * ITEMS // 2)

        @block.gpsimd
        def _(pool):
            pool.memset(v_all[:, :, :, :, HD:HD + 1], 1.0).then_inc(ones_set, 1)
            pool.wait_ge(ones_set, 1)

        @block.tensor
        def _(pe):
            pe.wait_ge(weights_in, 16 * WEIGHTS)
            with pe.Fori(0, NCH // 2) as cc:
                for p in range(2):
                    c = cc * 2 + p
                    pe.wait_ge(x_in[p], cc * 16 + 16)
                    for m in range(ITEMS):
                        ft, t = m // 2, m % 2
                        pe.wait_ge(qk_free, c * ITEMS + m + 1)
                        for r in range(2):
                            for i in range(FT):
                                last = pe.matmul(ps[m % 2][:, r], w_sb[:, 2 * t + r, i, ft * P:(ft + 1) * P],
                                                 xt[p][:, i], start=(i == 0), stop=(i == FT - 1))
                        last.then_inc(qk_ready, 1)
                    for a in range(2):
                        pe.wait_ge(v_free, c * 2 + a + 1)
                        for b in range(2):
                            tt = 2 * a + b
                            for i in range(FT):
                                last = pe.matmul(psv[a][:, b], xt[p][:, i, tt * P:(tt + 1) * P], wv_sb[:, i],
                                                 start=(i == 0), stop=(i == FT - 1))
                        last.then_inc(v_ready, 1)

        @block.vector
        def _(dve):
            dve.sem_inc(qk_free, 2)
            dve.sem_inc(v_free, 2)
            for b in range(2):
                dve.sem_inc(parts_free[b], 16)
            dve.wait_ge(weights_in, 16 * WEIGHTS)
            with dve.Fori(0, NCH // 2) as cc:
                for p in range(2):
                    c = cc * 2 + p
                    dve.wait_ge(table_in[p], cc * 16 * TABLES + 16 * TABLES)
                    for m in range(ITEMS):
                        ft, t, b = m // 2, m % 2, m % 2
                        base = (c * ITEMS + m) * STEPS
                        dve.wait_ge(qk_ready, c * ITEMS + m + 1)
                        dve.wait_ge(parts_free[b], (c * FT + ft) * 16 + 16)
                        dve.scalar_tensor_tensor(out=turned[b][:, 0], in0=ps[b][:, 0], scalar=b_sb[:, 2 * t, ft:ft + 1],
                                                 in1=table[p][:, 0], op0=ALU.add, op1=ALU.mult).then_inc(turn, 1)
                        dve.scalar_tensor_tensor(out=turned[b][:, 1], in0=ps[b][:, 1],
                                                 scalar=b_sb[:, 2 * t + 1, ft:ft + 1], in1=table[p][:, 1],
                                                 op0=ALU.add, op1=ALU.mult).then_inc(turn, 1)
                        dve.wait_ge(turn, base + 2)
                        dve.tensor_tensor(whole[b][:], turned[b][:, 0], turned[b][:, 1], ALU.add).then_inc(qk_free, 1)
                        dve.wait_ge(qk_free, c * ITEMS + m + 3)
                        dve.tensor_copy(parts[b][:, 0], whole[b][:]).then_inc(turn, 1)
                        dve.wait_ge(turn, base + 3)
                        dve.tensor_tensor(rest[b][:], whole[b][:], parts[b][:, 0], ALU.subtract).then_inc(turn, 1)
                        dve.wait_ge(turn, base + 4)
                        dve.tensor_copy(parts[b][:, 1], rest[b][:]).then_inc(turn, 1)
                        dve.wait_ge(turn, base + 5)
                        dve.tensor_tensor(parts[b][:, 2], rest[b][:], parts[b][:, 1], ALU.subtract).then_inc(turn, 1)
                    for a in range(2):
                        dve.wait_ge(v_ready, c * 2 + a + 1)
                        for b in range(2):
                            dst = v_all[:, :, bass.ds(c * TT + 2 * a + b, 1), :, 0:HD]
                            last = dve.tensor_tensor(dst.rearrange("p g a j d -> p (g a) j d"),
                                                     psv[a][:, b].rearrange("p (g j d) -> p g j d", g=NG, j=HG),
                                                     bv_sb[:].rearrange("p (g j d) -> p g j d", g=NG, j=HG), ALU.add)
                        last.then_inc(v_free, 1)
            dve.wait_ge(v_free, 2 + 2 * NCH)


def attend(nc, io, parts_dram, heads_dram, v_all):
    with ExitStack() as ctx:
        def sb(name, shape, dt=F32):
            return ctx.enter_context(nc.sbuf_tensor(name, shape, dt))

        def psum(name, shape):
            return ctx.enter_context(nc.psum_tensor(name, shape, F32))

        def sem(name):
            return ctx.enter_context(nc.semaphore(name))

        RING, BANKS = 8, 3
        QT = HG * TT
        WIDE = 2 * CH
        MAXG = QT * S // WIDE
        SLOTS = KT * HG
        UNITS = NCH * NG
        FREE_OF_MAX = 2
        ROUNDS = 4

        k_all = sb("k_all", [ROWS, NG, HG, S], BF16)
        q_sb = [sb(f"q_sb{g}", [ROWS, HG, CH], BF16) for g in range(NG)]
        probs = [sb(f"probs{r}", [P, CH]) for r in range(RING)]
        mixed = [sb(f"mixed{p}", [P, CH]) for p in range(2)]
        ident = sb("ident", [P, P])
        group_max = sb("group_max", [P, MAXG])
        top = sb("top", [P, QT])
        top_rest = sb("top_rest", [QT, P])
        top_parts = sb("top_parts", [QT, 3, P], BF16)
        scores = [psum(f"scores{b}", [P, CH]) for b in range(BANKS)]
        wide = [psum(f"wide{b}", [P, 2, CH]) for b in range(2)]
        sums = psum("sums", [P, CH])

        k_in = [sem(f"k_in{g}") for g in range(NG)]
        q_in = [sem(f"q_in{g}") for g in range(NG)]
        k_ones = sem("k_ones")
        ident_set = sem("ident_set")
        wide_ready = sem("wide_ready")
        wide_free = sem("wide_free")
        max_step = sem("max_step")
        shift_in = sem("shift_in")
        scored = sem("scored")
        exps_done = sem("exps_done")
        probs_free = sem("probs_free")
        sums_free = sem("sums_free")
        mixed_free = [sem(f"mixed_free{p}") for p in range(2)]

        spread = SLOTS - FREE_OF_MAX * HG
        before = [n * MAXG // spread for n in range(spread)] + [MAXG] * (SLOTS - spread + 1)
        TURNS = MAXG + 2

        block = ctx.enter_context(nc.Block())

        @block.sync
        def _(sp):
            def load_q(c, g):
                for r in range(NPROD):
                    src = parts_dram[0][Q_PART[r]].rearrange("(h d) s -> d h s", d=HD)[:, g * HG:(g + 1) * HG]
                    sp.dma_start(q_sb[g][r * HD:(r + 1) * HD], src[:, :, bass.ds(c * CH, CH)]).then_inc(q_in[g], 16)

            def place_shift(u, g):
                sp.wait_ge(max_step, u * ROUNDS + ROUNDS)
                for a in range(3):
                    row = q_sb[g][SHIFT_ROW + a:SHIFT_ROW + a + 1].rearrange("o j (t s) -> o (j t) s", t=TT)
                    sp.dma_start(row, top_parts[:, a]).then_inc(shift_in, 16)

            def finish(c, g):
                sp.wait_ge(sums_free, c * NG + g + 2)
                sp.dma_start(heads_dram[bass.ds(c, 1), :, g].rearrange("c p s -> (c p) s"), mixed[g % 2][:])\
                    .then_inc(mixed_free[g % 2], 16)

            for g in range(NG):
                load_q(0, g)
                for r in range(NPROD):
                    src = parts_dram[1][K_PART[r]].rearrange("(h d) s -> d h s", d=HD)[:, g * HG:(g + 1) * HG]
                    sp.dma_start(k_all[r * HD:(r + 1) * HD, g], src).then_inc(k_in[g], 16)
            place_shift(0, 0)
            with sp.Fori(0, NCH - 1) as c:
                for g in range(NG):
                    place_shift(c * NG + g + 1, (g + 1) % NG)
                    finish(c, g)
                    load_q(c + 1, g)
            for g in range(NG):
                if g < NG - 1:
                    place_shift((NCH - 1) * NG + g + 1, g + 1)
                finish(NCH - 1, g)
            for p in range(2):
                sp.wait_ge(mixed_free[p], 16 + 16 * UNITS // 2)

        @block.gpsimd
        def _(pool):
            pool.memset(ident[:], 0.0).then_inc(ident_set, 1)
            pool.wait_ge(ident_set, 1)
            pool.affine_select(out=ident[:], in_=ident[:], compare_op=ALU.not_equal, fill=1.0, base=0,
                               pattern=[[-1, P]], channel_multiplier=1).then_inc(ident_set, 1)
            pool.wait_ge(ident_set, 2)
            for g in range(NG):
                pool.memset(k_all[SHIFT_ROW:ROWS, g], 1.0).then_inc(k_ones, 1)
                pool.wait_ge(k_ones, g + 1)

        @block.tensor
        def _(pe):
            def max_group(u, g, n):
                j, t, b = n // (TT * 4), n // 4 % TT, n % 4
                pe.wait_ge(wide_free, u * TURNS + n + 1)
                for h in range(2):
                    keys = slice((2 * b + h) * CH, (2 * b + h + 1) * CH)
                    last = pe.matmul(wide[n % 2][:, h], q_sb[g][0:SHIFT_ROW, j, t * P:(t + 1) * P],
                                     k_all[0:SHIFT_ROW, g, j, keys], start=True, stop=True)
                last.then_inc(wide_ready, 1)

            def max_turn(u):
                pe.wait_ge(max_step, u * ROUNDS + 1)
                pe.transpose(wide[0][0:QT, 0, 0:P], top[:], ident[:]).then_inc(wide_ready, 1)

            def max_start(c, g):
                pe.wait_ge(q_in[g], c * (16 * NPROD) + 16 * NPROD)
                pe.wait_ge(k_in[g], 16 * NPROD)

            def sum_over(u, g, kt):
                if kt == 0:
                    pe.wait_ge(sums_free, u + 1)
                pe.wait_ge(exps_done, u * SLOTS + (kt + 1) * HG + BANKS)
                for j in range(HG):
                    last = pe.matmul(sums[32 * j:32 * j + HD + 1, :], v_all[:, g, kt, j], probs[(kt * HG + j) % RING][:],
                                     start=(kt == 0), stop=(kt == KT - 1))
                last.then_inc(probs_free, 1)

            def unit(c, g, more=True):
                u = c * NG + g
                if more:
                    g1, c1 = (g + 1) % NG, c + (g + 1) // NG
                    max_start(c1, g1)
                pe.wait_ge(shift_in, u * 48 + 96)
                for n in range(SLOTS):
                    kt, j = n // HG, n % HG
                    pe.wait_ge(exps_done, u * SLOTS + max(n + 1, min(n + 2, BANKS)))
                    pe.matmul(scores[n % BANKS][:], k_all[:, g, j, kt * P:(kt + 1) * P], q_sb[g][:, j],
                              start=True, stop=True).then_inc(scored, 1)
                    if more:
                        for m in range(before[n], before[n + 1]):
                            max_group(u + 1, g1, m)
                        if n == spread + 3:
                            max_turn(u + 1)
                    if j == HG - 1 and kt > 0:
                        sum_over(u, g, kt - 1)
                sum_over(u, g, KT - 1)

            pe.wait_ge(ident_set, 2)
            pe.wait_ge(k_ones, NG)
            max_start(0, 0)
            for n in range(MAXG):
                max_group(0, 0, n)
            max_turn(0)
            with pe.Fori(0, NCH - 1) as c:
                for g in range(NG):
                    unit(c, g)
            for g in range(NG):
                unit(NCH - 1, g, more=g < NG - 1)

        @block.scalar
        def _(act):
            act.sem_inc(exps_done, BANKS)
            act.sem_inc(probs_free, RING // HG)
            with act.Fori(0, NCH) as c:
                for g in range(NG):
                    u = c * NG + g
                    for n in range(SLOTS):
                        act.wait_ge(scored, u * SLOTS + n + 1)
                        if n % HG == 0:
                            act.wait_ge(probs_free, u * KT + n // HG + 1)
                        act.activation(probs[n % RING][:], scores[n % BANKS][:], ACT.Exp, scale=INV_SCALE)\
                            .then_inc(exps_done, 1)
                    act.wait_ge(probs_free, (u + 1) * KT + RING // HG)
                    act.wait_ge(mixed_free[g % 2], (c * 2 + g // 2) * 16 + 16)
                    act.activation(mixed[g % 2][:], sums[:], ACT.Copy).then_inc(sums_free, 1)

        @block.vector
        def _(dve):
            def maxima(u):
                for n in range(MAXG):
                    dve.wait_ge(wide_ready, u * (MAXG + 1) + n + 1)
                    dve.reduce_max(group_max[:, n:n + 1], wide[n % 2][:], mybir.AxisListType.XY).then_inc(wide_free, 1)
                dve.wait_ge(wide_free, u * TURNS + MAXG + 2)
                dve.reduce_max(top[:], group_max[:].rearrange("q (r b) -> q r b", b=4), AX_X).then_inc(max_step, 1)
                dve.wait_ge(wide_ready, (u + 1) * (MAXG + 1))
                dve.wait_ge(shift_in, u * 48 + 48)
                turned = wide[0][0:QT, 0, 0:P]
                dve.tensor_scalar(top_parts[:, 0], turned, -1.0, None, ALU.mult).then_inc(max_step, 1)
                dve.wait_ge(max_step, u * ROUNDS + 2)
                dve.scalar_tensor_tensor(out=top_rest[:], in0=turned, scalar=-1.0, in1=top_parts[:, 0],
                                         op0=ALU.mult, op1=ALU.subtract).then_inc(wide_free, 2)
                dve.wait_ge(wide_free, (u + 1) * TURNS + 2)
                dve.tensor_copy(top_parts[:, 1], top_rest[:]).then_inc(max_step, 1)
                dve.wait_ge(max_step, u * ROUNDS + 3)
                dve.tensor_tensor(top_parts[:, 2], top_rest[:], top_parts[:, 1], ALU.subtract).then_inc(max_step, 1)

            for p in range(2):
                dve.sem_inc(mixed_free[p], 16)
            dve.sem_inc(wide_free, 2)
            dve.sem_inc(shift_in, 48)
            dve.memset(sums[:], 0.0).then_inc(sums_free, 1)
            maxima(0)
            with dve.Fori(1, UNITS) as u:
                maxima(u)


def feed_forward(nc, io, heads_dram, out):
    with ExitStack() as ctx:
        def sb(name, shape, dt=F32):
            return ctx.enter_context(nc.sbuf_tensor(name, shape, dt))

        def psum(name, shape):
            return ctx.enter_context(nc.psum_tensor(name, shape, F32))

        def sem(name):
            return ctx.enter_context(nc.semaphore(name))

        wo = sb("wo", [P, NG, D])
        w1, w2 = sb("w1", [P, FT, HID]), sb("w2", [P, FT, HID])
        h1, h2 = sb("h1", [P, HT, HID]), sb("h2", [P, HT, HID])
        w3 = sb("w3", [P, HT, D])
        scale = sb("scale", [P, 4, HT])
        scale3 = sb("scale3", [P, D])
        ident = sb("ident_ff", [P, P])
        heads = [sb(f"heads{p}", [P, NG, CH]) for p in range(2)]
        shares = sb("shares", [P, NG, CH])
        x_sb = [sb(f"x_sb{p}", [P, TT, D]) for p in range(2)]
        x1 = [sb(f"x1_{p}", [P, TT, D]) for p in range(2)]
        x1t = [sb(f"x1t{p}", [P, FT, CH]) for p in range(2)]
        hid_a, hid_b = sb("hid_a", [P, HT, CH]), sb("hid_b", [P, HT, CH])
        gate = [sb(f"gate{b}", [P, CH]) for b in range(4)]
        fin = [sb(f"fin{p}", [P, TT, D]) for p in range(2)]
        stats = [sb(f"stats{i}", [P, TT, 6]) for i in range(2)]
        moments = [sb(f"moments{i}", [P, TT, 2]) for i in range(2)]
        spread = [sb(f"spread{i}", [P, TT]) for i in range(2)]
        root = [sb(f"root{i}", [P, TT]) for i in range(2)]
        inverse = [sb(f"inverse{i}", [P, TT]) for i in range(2)]
        acc = [psum(f"acc{b}", [P, CH]) for b in range(4)]
        tok = [psum(f"tok{b}", [P, 2, D]) for b in range(2)]
        flip = [psum(f"flip{b}", [P, CH]) for b in range(2)]

        weights_in = sem("ff_weights_in")
        heads_in = [sem(f"heads_in{p}") for p in range(2)]
        x_ff_in = [sem(f"x_ff_in{p}") for p in range(2)]
        wo_zero = sem("wo_zero")
        ident_set = sem("ident_ff_set")
        acc_ready = sem("acc_ready")
        gated = sem("gated")
        hid_ready = sem("hid_ready")
        tok_ready = sem("tok_ready")
        share_step = sem("share_step")
        norm1 = sem("norm1")
        norm2 = sem("norm2")
        root_done = sem("root_done")
        flip_ready = sem("flip_ready")
        x1t_ready = sem("x1t_ready")
        waited = sem("ff_waited")
        fin_free = [sem(f"fin_free{p}") for p in range(2)]

        ACCS = 4 * HT
        HIDS = 3 * HT
        NORM1 = 4 * TT + 2
        NORM2 = 5 * TT + 2
        WEIGHTS = HG + 4 + 5 + 1

        block = ctx.enter_context(nc.Block())

        @block.sync
        def _(sp):
            def load(c, p):
                sp.dma_start(heads[p][:], heads_dram[bass.ds(c, 1)].rearrange("c p g s -> (c p) g s"))\
                    .then_inc(heads_in[p], 16)
                sp.dma_start(x_sb[p][:], io["x"].rearrange("(c t p) d -> c p t d", t=TT, p=P)[bass.ds(c, 1)]
                             .rearrange("c p t d -> (c p) t d")).then_inc(x_ff_in[p], 16)

            def store(c, p):
                sp.wait_ge(norm2, (c + 2) * NORM2)
                sp.dma_start(out.rearrange("(c t p) d -> c p t d", t=TT, p=P)[bass.ds(c, 1)]
                             .rearrange("c p t d -> (c p) t d"), fin[p][:]).then_inc(fin_free[p], 16)

            sp.wait_ge(wo_zero, 1)
            for j in range(HG):
                sp.dma_start(wo[32 * j:32 * j + HD], io["woT"].rearrange("(g j d) o -> j d g o", g=NG, j=HG)[j])\
                    .then_inc(weights_in, 16)
            load(0, 0)
            for n, name in enumerate(["w1_s", "w2_s", "h1_s", "h2_s"]):
                sp.dma_start(scale[:, n], io[name]).then_inc(weights_in, 16)
            for dst, name in [(w1, "w1T"), (w2, "w2T"), (h1, "h1T"), (h2, "h2T"), (w3, "w3T")]:
                sp.dma_start(dst[:], io[name].rearrange("(t p) o -> p t o", p=P)).then_inc(weights_in, 16)
            sp.dma_start(scale3[:], io["w3_s"].partition_broadcast(P)).then_inc(weights_in, 16)
            load(1, 1)
            with sp.Fori(0, NCH // 2 - 1) as cc:
                for p in range(2):
                    c = cc * 2 + p
                    store(c, p)
                    load(c + 2, p)
            for p in range(2):
                store(NCH - 2 + p, p)
            for p in range(2):
                sp.wait_ge(fin_free[p], 16 + 16 * NCH // 2)

        @block.gpsimd
        def _(pool):
            pool.memset(wo[:], 0.0).then_inc(wo_zero, 1)
            pool.wait_ge(wo_zero, 1)
            pool.memset(ident[:], 0.0).then_inc(ident_set, 1)
            pool.wait_ge(ident_set, 1)
            pool.affine_select(out=ident[:], in_=ident[:], compare_op=ALU.not_equal, fill=1.0, base=0,
                               pattern=[[-1, P]], channel_multiplier=1).then_inc(ident_set, 1)

        def front_turn(c):
            return 0 if isinstance(c, int) and c == 0 else c * 2 - 1

        def back_turn(c, last):
            return c * 2 + 1 if last else c * 2 + 2

        @block.tensor
        def _(pe):
            def front(c, half, p):
                pe.wait_ge(share_step, c * 3 + 3)
                for t in range(TT):
                    if t % 2 == 0 and not (isinstance(c, int) and c == 0):
                        pe.wait_ge(norm2, (c - 1) * NORM2 + t + 2)
                    for g in range(NG):
                        last = pe.matmul(tok[t // 2][:, t % 2], heads[p][:, g, t * P:(t + 1) * P], wo[:, g],
                                         start=(g == 0), stop=(g == NG - 1))
                    if t % 2 == 1:
                        last.then_inc(tok_ready, 1)

            def front_flip(c, p):
                pe.wait_ge(norm1, (c + 1) * NORM1)
                for f in range(FT):
                    for t in range(TT):
                        last = pe.transpose(flip[f][:, t * P:(t + 1) * P], x1[p][:, t, f * P:(f + 1) * P], ident[:])
                    last.then_inc(flip_ready, 1)

            def acc_read(c, n):
                if n < 2 * HT and n % 2 == 0:
                    pe.wait_ge(gated, c * HT + n // 2 + 1)
                elif n < 2 * HT:
                    pe.wait_ge(hid_ready, c * HIDS + n // 2 + 1)
                else:
                    pe.wait_ge(hid_ready, c * HIDS + (n - HT) + 1)

            def gate_layer(c, p):
                pe.wait_ge(x1t_ready, (c + 1) * FT)
                for o in range(HT):
                    for w, wt in enumerate((w1, w2)):
                        n = 2 * o + w
                        if n >= 4:
                            acc_read(c, n - 4)
                        for i in range(FT):
                            last = pe.matmul(acc[n % 4][:], wt[:, i, o * P:(o + 1) * P], x1t[p][:, i],
                                             start=(i == 0), stop=(i == FT - 1))
                        last.then_inc(acc_ready, 1)

            def hidden_layer(c, layer):
                src, wt = ((hid_a, h1), (hid_b, h2))[layer]
                for o in range(HT):
                    n = (2 + layer) * HT + o
                    acc_read(c, n - 4)
                    for i in range(HT):
                        if o == 0:
                            pe.wait_ge(hid_ready, c * HIDS + layer * HT + i + 1)
                        last = pe.matmul(acc[n % 4][:], wt[:, i, o * P:(o + 1) * P], src[:, i],
                                         start=(i == 0), stop=(i == HT - 1))
                    last.then_inc(acc_ready, 1)

            def back(c, final):
                pe.wait_ge(hid_ready, (c + 1) * HIDS)
                for t in range(TT):
                    if t % 2 == 0 and final:
                        pe.wait_ge(norm2, c * NORM2 + t + 2)
                    for i in range(HT):
                        last = pe.matmul(tok[t // 2][:, t % 2], hid_a[:, i, t * P:(t + 1) * P], w3[:, i],
                                         start=(i == 0), stop=(i == HT - 1))
                    if t % 2 == 1:
                        last.then_inc(tok_ready, 1)

            def chunk(half, p, final=False):
                c = half * 2 + p
                gate_layer(c, p)
                if not final:
                    front(c + 1, half + p, 1 - p)
                hidden_layer(c, 0)
                if not final:
                    front_flip(c + 1, 1 - p)
                hidden_layer(c, 1)
                back(c, final)

            pe.wait_ge(ident_set, 2)
            pe.wait_ge(weights_in, 16 * WEIGHTS)
            front(0, 0, 0)
            front_flip(0, 0)
            with pe.Fori(0, NCH // 2 - 1) as half:
                for p in range(2):
                    chunk(half, p)
            chunk(NCH // 2 - 1, 0)
            chunk(NCH // 2 - 1, 1, final=True)

        @block.scalar
        def _(act):
            def front_root(c):
                act.wait_ge(norm1, c * NORM1 + 3 * TT + 1)
                act.activation(root[0][:], spread[0][:], ACT.Sqrt).then_inc(root_done, 1)

            def front_flip(c, p):
                for f in range(FT):
                    act.wait_ge(flip_ready, c * FT + f + 1)
                    act.activation(x1t[p][:, f], flip[f][:], ACT.Copy).then_inc(x1t_ready, 1)

            def gates(c):
                for o in range(HT):
                    act.wait_ge(acc_ready, c * ACCS + 2 * o + 1)
                    if o >= 4:
                        act.wait_ge(hid_ready, c * HIDS + o - 3)
                    act.activation(gate[o % 4][:], acc[(2 * o) % 4][:], ACT.Silu, scale=scale[:, 0, o:o + 1])\
                        .then_inc(gated, 1)

            def gelus(c, layer):
                dst = (hid_b, hid_a)[layer]
                for o in range(HT):
                    n = (2 + layer) * HT + o
                    act.wait_ge(acc_ready, c * ACCS + n + 1)
                    act.activation(dst[:, o], acc[n % 4][:], ACT.Gelu, scale=scale[:, 2 + layer, o:o + 1])\
                        .then_inc(hid_ready, 1)

            def back_root(c):
                act.wait_ge(norm2, (c + 1) * NORM2 + 4 * TT + 1)
                act.activation(root[1][:], spread[1][:], ACT.Sqrt).then_inc(root_done, 1)

            def chunk(half, p, final=False):
                c = half * 2 + p
                gates(c)
                if not final:
                    front_root(c + 1)
                gelus(c, 0)
                if not final:
                    front_flip(c + 1, 1 - p)
                gelus(c, 1)
                back_root(c)

            act.wait_ge(weights_in, 16 * WEIGHTS)
            front_root(0)
            front_flip(0, 0)
            with act.Fori(0, NCH // 2 - 1) as half:
                for p in range(2):
                    chunk(half, p)
            chunk(NCH // 2 - 1, 0)
            chunk(NCH // 2 - 1, 1, final=True)

        @block.vector
        def _(dve):
            def normalise(i, data, dst, done, base, turn):
                for t in range(TT):
                    dve.wait_ge(done, base - TT + t + 1)
                    dve.bn_stats(stats[i][:, t], data[:, t]).then_inc(done, 1)
                for t in range(TT):
                    dve.wait_ge(done, base + t + 1)
                    dve.sem_inc(waited, 1)
                    dve.bn_aggr(moments[i][:, t], stats[i][:, t]).then_inc(done, 1)
                dve.wait_ge(done, base + 2 * TT)
                dve.tensor_scalar(spread[i][:], moments[i][:, :, 1], EPS, None, ALU.add).then_inc(done, 1)
                dve.wait_ge(root_done, turn + 1)
                dve.reciprocal(inverse[i][:], root[i][:]).then_inc(done, 1)
                dve.wait_ge(done, base + 2 * TT + 2)
                for t in range(TT):
                    dve.tensor_scalar(dst[:, t], data[:, t], moments[i][:, t, 0:1], inverse[i][:, t:t + 1],
                                      ALU.subtract, ALU.mult).then_inc(done, 1)

            def divide(c, half, p):
                dve.wait_ge(heads_in[p], half * 16 + 16)
                dve.sem_inc(waited, 1)
                dve.stream_shuffle(shares[:], heads[p][:], [HD] * 32).then_inc(share_step, 1)
                dve.wait_ge(share_step, c * 3 + 1)
                dve.reciprocal(shares[:], shares[:]).then_inc(share_step, 1)
                dve.wait_ge(share_step, c * 3 + 2)
                dve.tensor_tensor(heads[p][:], heads[p][:], shares[:], ALU.mult).then_inc(share_step, 1)

            def front(c, half, p):
                turn = front_turn(c)
                dve.wait_ge(x_ff_in[p], half * 16 + 16)
                for t in range(TT):
                    if t % 2 == 0:
                        dve.wait_ge(tok_ready, turn * 2 + t // 2 + 1)
                    dve.tensor_tensor(x1[p][:, t], tok[t // 2][:, t % 2], x_sb[p][:, t], ALU.add).then_inc(norm1, 1)
                normalise(0, x1[p], x1[p], norm1, c * NORM1 + TT, turn)

            def gates(c):
                for o in range(HT):
                    dve.wait_ge(gated, c * HT + o + 1)
                    dve.wait_ge(acc_ready, c * ACCS + 2 * o + 2)
                    dve.scalar_tensor_tensor(out=hid_a[:, o], in0=acc[(2 * o + 1) % 4][:], scalar=scale[:, 1, o:o + 1],
                                             in1=gate[o % 4][:], op0=ALU.mult, op1=ALU.mult).then_inc(hid_ready, 1)

            def back(c, half, p, final):
                turn, base = back_turn(c, final), (c + 1) * NORM2
                dve.wait_ge(fin_free[p], half * 16 + 16)
                for t in range(TT):
                    if t % 2 == 0:
                        dve.wait_ge(tok_ready, turn * 2 + t // 2 + 1)
                    dve.tensor_tensor(fin[p][:, t], tok[t // 2][:, t % 2], scale3[:], ALU.mult).then_inc(norm2, 1)
                for t in range(TT):
                    dve.wait_ge(norm2, base + t + 1)
                    dve.tensor_tensor(fin[p][:, t], fin[p][:, t], x1[p][:, t], ALU.add).then_inc(norm2, 1)
                normalise(1, fin[p], fin[p], norm2, base + 2 * TT, turn)

            def chunk(half, p, final=False):
                c = half * 2 + p
                if not final:
                    divide(c + 1, half + p, 1 - p)
                gates(c)
                if not final:
                    front(c + 1, half + p, 1 - p)
                back(c, half, p, final)

            dve.sem_inc(norm2, NORM2)
            for p in range(2):
                dve.sem_inc(fin_free[p], 16)
            dve.wait_ge(weights_in, 16 * WEIGHTS)
            divide(0, 0, 0)
            front(0, 0, 0)
            with dve.Fori(0, NCH // 2 - 1) as half:
                for p in range(2):
                    chunk(half, p)
            chunk(NCH // 2 - 1, 0)
            chunk(NCH // 2 - 1, 1, final=True)


def build(nc, io, out):
    parts_dram = [nc.dram_tensor(f"{t}_parts", [3, D, S], BF16, kind="Internal").ap() for t in "qk"]
    heads_dram = nc.dram_tensor("heads", [NCH, P, NG, CH], F32, kind="Internal").ap()
    with nc.sbuf_tensor("v_all", [P, NG, KT, HG, HD + 1], F32) as v_all:
        project(nc, io, parts_dram, v_all)
        attend(nc, io, parts_dram, heads_dram, v_all)
    feed_forward(nc, io, heads_dram, out)


def kernel(**inputs):
    import numpy as np
    import concourse.bacc as bacc
    from concourse.bass_utils import run_bass_kernel_spmd

    a = {k.removeprefix("L0_"): np.asarray(v) for k, v in inputs.items()}
    pair = np.arange(D).reshape(D // 2, 2)[:, ::-1].reshape(D)

    def columns(v):
        return v.reshape(-1, P).T

    freqs = np.float32(10000.0) ** (-np.arange(0, HD, 2).astype(np.float32) / np.float32(HD))
    angle = np.arange(S, dtype=np.float32)[:, None] * freqs[None, :]
    cos, sin = np.cos(angle), np.sin(angle)
    cos_rows = np.stack([cos, cos], axis=-1).reshape(S, HD).T
    sin_rows = np.stack([-sin, sin], axis=-1).reshape(S, HD).T

    arrays = {
        "x": a["attn_x"][0], "xT": a["attn_x"][0].T,
        "wqT": a["attn_Wq"].T, "wqrT": a["attn_Wq"][pair].T, "wkT": a["attn_Wk"].T, "wkrT": a["attn_Wk"][pair].T,
        "wvT": a["attn_Wv"].T, "woT": a["attn_Wo"].T,
        "bq": columns(a["attn_bq"]), "bqr": columns(a["attn_bq"][pair]),
        "bk": columns(a["attn_bk"]), "bkr": columns(a["attn_bk"][pair]), "bv": a["attn_bv"],
        "cos": cos_rows, "sin": sin_rows,
        "w1T": a["ffn_w1_w"].T, "w2T": a["ffn_w2_w"].T, "h1T": a["ffn_h1_w"].T, "h2T": a["ffn_h2_w"].T,
        "w3T": a["ffn_w3_w"].T,
        "w1_s": columns(a["ffn_w1_s"]), "w2_s": columns(a["ffn_w2_s"]),
        "h1_s": columns(a["ffn_h1_s"]), "h2_s": columns(a["ffn_h2_s"]), "w3_s": a["ffn_w3_s"],
    }
    arrays = {k: np.ascontiguousarray(v) for k, v in arrays.items()}
    nc = bacc.Bacc("TRN2", target_bir_lowering=False, num_devices=1)
    io = {k: nc.dram_tensor(f"in_{k}", v.shape, mybir.dt.from_np(v.dtype), kind="ExternalInput").ap()
          for k, v in arrays.items()}
    out = nc.dram_tensor("out_0", [S, D], F32, kind="ExternalOutput").ap()
    build(nc, io, out)
    r = run_bass_kernel_spmd(nc, [{f"in_{k}": v for k, v in arrays.items()}], core_ids=[0])
    return r.results[0]["out_0"].reshape(1, S, D)
```

```python
from contextlib import ExitStack

import concourse.bass as bass
from concourse import mybir

F32 = mybir.dt.float32
F32R = mybir.dt.float32r
BF16 = mybir.dt.bfloat16
I32 = mybir.dt.int32
ALU = mybir.AluOpType
ACT = mybir.ActivationFunctionType
AX_X = mybir.AxisListType.X

P = 128
S, D, H = 4096, 256, 16
HD = D // H
HID = 1024
CH = 512
NCH = S // CH
TT = CH // P
NG = 4
HG = H // NG
KT = S // P
FT = D // P
HT = HID // P
EPS = 1e-5
LOW_BITS = 0xFFF

W_SHAPES = {"w1T": (D, HID), "w2T": (D, HID), "h1T": (HID, HID), "h2T": (HID, HID), "w3T": (HID, D)}
W_AT, W_TOTAL = {}, 0
for _name, (_rows, _cols) in W_SHAPES.items():
    W_AT[_name] = (W_TOTAL, _rows, _cols)
    W_TOTAL += _rows * _cols
INV_SCALE = 1.0 / float(D) ** 0.5

K_PART = [0, 1, 2, 0, 1, 0]
Q_PART = [0, 0, 0, 1, 1, 2]
NPROD = len(K_PART)
SHIFT_ROW = NPROD * HD
ROWS = SHIFT_ROW + 3


def place_k(sp, k_parts, k_all, c, ft, done):
    groups = NG // FT
    for r in range(NPROD):
        src = k_parts[K_PART[r]].rearrange("(h d) s -> d h s", d=HD)
        src = src[:, ft * groups * HG:(ft + 1) * groups * HG, bass.ds(c * CH, CH)]
        dst = k_all[r * HD:(r + 1) * HD, ft * groups:(ft + 1) * groups, :, bass.ds(c * CH, CH)]
        sp.dma_start(dst.rearrange("d g j s -> d (g j) s"), src).then_inc(done, 16)


def place_q(sp, q_parts, q_sb, c, g, done):
    for r in range(NPROD):
        src = q_parts[Q_PART[r]].rearrange("(h d) s -> d h s", d=HD)[:, g * HG:(g + 1) * HG]
        sp.dma_start(q_sb[r * HD:(r + 1) * HD], src[:, :, bass.ds(c * CH, CH)]).then_inc(done, 16)


def project(nc, io, parts_dram, v_all, k_all, first_q):
    with ExitStack() as ctx:
        def sb(name, shape, dt=F32):
            return ctx.enter_context(nc.sbuf_tensor(name, shape, dt))

        def psum(name, shape):
            return ctx.enter_context(nc.psum_tensor(name, shape, F32))

        def sem(name):
            return ctx.enter_context(nc.semaphore(name))

        RING = 4
        w_sb = sb("w_qk", [P, 2, FT, D])
        wv_sb = sb("w_v", [P, FT, D])
        b_sb = sb("b_qk", [P, 2, FT])
        bv_sb = sb("b_v", [1, D])
        one_row = sb("one_row", [1, P])
        xt = [sb(f"xt{p}", [P, FT, CH]) for p in range(2)]
        table = [sb(f"table{p}", [P, 2, CH]) for p in range(2)]
        item = [sb(f"item{b}", [P, CH]) for b in range(RING)]
        pair = [sb(f"pair{b}", [P, CH]) for b in range(2)]
        parts = [sb(f"parts{b}", [P, 3, CH], BF16) for b in range(2)]
        ps = [psum(f"ps_qk{b}", [P, CH]) for b in range(RING)]
        psv = [psum(f"ps_v{a}", [P, 2, D]) for a in range(2)]

        w_in = sem("w_qk_in")
        b_in = sem("b_qk_in")
        v_weights_in = sem("v_weights_in")
        x_in = [sem(f"x_in{p}") for p in range(2)]
        table_in = [sem(f"table_in{p}") for p in range(2)]
        projected = sem("projected")
        biased = sem("biased")
        swapped = sem("swapped")
        sine_done = sem("sine_done")
        cosine_done = sem("cosine_done")
        rotated = sem("rotated")
        high_done = sem("high_done")
        rest_done = sem("rest_done")
        middle_done = sem("middle_done")
        low_done = sem("low_done")
        parts_free = [sem(f"parts_free{b}") for b in range(2)]
        first_q_in = sem("first_q_in")
        k_in = sem("k_in")
        v_ready = sem("v_ready")
        v_free = sem("v_free")
        waited = sem("project_waited")
        sp_waited = sem("sp_waited")
        ones_set = sem("ones_set")

        ITEMS = 2 * FT
        TOTAL = NCH * ITEMS

        def started(n):
            return not isinstance(n, int) or 0 <= n < TOTAL

        block = ctx.enter_context(nc.Block())

        @block.sync
        def _(sp):
            def load(p, c):
                cols = bass.ds(c * CH, CH)
                sp.dma_start(xt[p][:], io["xT"].rearrange("(t p) s -> p t s", p=P)[:, :, cols]).then_inc(x_in[p], 16)
                for n, name in enumerate(["cos", "sin"]):
                    sp.dma_start(table[p][:, n], io[name][:, cols]).then_inc(table_in[p], 16)

            def store(c, m):
                ft, t = m // 2, m % 2
                sp.wait_ge(low_done, RING + c * ITEMS + m + 1)
                dst = parts_dram[t].rearrange("a f s -> f a s")[ft * P:(ft + 1) * P]
                sp.dma_start(dst[:, :, bass.ds(c * CH, CH)], parts[t][:]).then_inc(parts_free[t], 16)

            def place(c, ft):
                sp.wait_ge(parts_free[1], 16 + (c * FT + ft + 1) * 16)
                sp.sem_inc(sp_waited, 1)
                place_k(sp, parts_dram[1], k_all, c, ft, k_in)

            def chunk(c, first=False):
                store(c, 0)
                if not first:
                    place(c - 1, 1)
                store(c, 1)
                store(c, 2)
                place(c, 0)
                store(c, 3)

            sp.dma_start(w_sb[:, 0], io["wqT"].rearrange("(t p) o -> p t o", p=P)).then_inc(w_in, 16)
            load(0, 0)
            for n, name in enumerate(["bq", "bk"]):
                sp.dma_start(b_sb[:, n], io[name]).then_inc(b_in, 16)
            sp.wait_ge(w_in, 16)
            sp.dma_start(w_sb[:, 1], io["wkT"].rearrange("(t p) o -> p t o", p=P)).then_inc(w_in, 16)
            sp.dma_start(wv_sb[:], io["wvT"].rearrange("(t p) o -> p t o", p=P)).then_inc(v_weights_in, 16)
            sp.dma_start(bv_sb[:], io["bv"].rearrange("(o d) -> o d", o=1)).then_inc(v_weights_in, 16)
            load(1, 1)
            chunk(0, first=True)
            sp.wait_ge(v_ready, 2)
            load(0, 2)
            chunk(1)
            sp.wait_ge(v_ready, 4)
            load(1, 3)
            with sp.Fori(1, NCH // 2 - 1) as cc:
                for p in range(2):
                    chunk(cc * 2 + p)
                    sp.wait_ge(v_ready, (cc * 2 + p + 1) * 2)
                    load(p, cc * 2 + p + 2)
            chunk(NCH - 2)
            sp.wait_ge(parts_free[0], 32)
            place_q(sp, parts_dram[0], first_q, 0, 0, first_q_in)
            chunk(NCH - 1)
            for b in range(2):
                sp.wait_ge(parts_free[b], 16 + 16 * TOTAL // 2)
            sp.wait_ge(first_q_in, 16 * NPROD)
            sp.wait_ge(k_in, 16 * NPROD * (NCH * FT - 1))

        @block.gpsimd
        def _(pool):
            pool.memset(v_all[:, :, :, :, HD:HD + 1], 1.0).then_inc(ones_set, 1)
            pool.wait_ge(ones_set, 1)
            pool.memset(one_row[:], 1.0).then_inc(ones_set, 1)
            pool.wait_ge(ones_set, 2)
            with pool.Fori(0, NCH // 2) as cc:
                for p in range(2):
                    pool.wait_ge(table_in[p], cc * 32 + 32)
                    for m in range(ITEMS):
                        n = (cc * 2 + p) * ITEMS + m
                        pool.wait_ge(swapped, n + 1)
                        pool.tensor_tensor(pair[m % 2][:], pair[m % 2][:], table[p][:, 1], ALU.mult).then_inc(sine_done, 1)

        @block.tensor
        def _(pe):
            def chunk(c, p):
                for m in range(ITEMS):
                    ft, t = m // 2, m % 2
                    n = c * ITEMS + m
                    if isinstance(c, int) and c == 0 and m < 2:
                        pe.wait_ge(w_in, 16 * (t + 1))
                    if started(n - RING):
                        pe.wait_ge(biased, n - RING + 1)
                    for i in range(FT):
                        last = pe.matmul(ps[m][:], w_sb[:, t, i, ft * P:(ft + 1) * P], xt[p][:, i],
                                         start=(i == 0), stop=(i == FT - 1))
                    last.then_inc(projected, 1)
                if isinstance(c, int) and c == 0:
                    pe.wait_ge(v_weights_in, 32)
                    pe.wait_ge(ones_set, 2)
                for a in range(2):
                    pe.wait_ge(v_free, c * 2 + a + 1)
                    for b in range(2):
                        tt = 2 * a + b
                        for i in range(FT):
                            pe.matmul(psv[a][:, b], xt[p][:, i, tt * P:(tt + 1) * P], wv_sb[:, i],
                                      start=(i == 0), stop=False)
                        last = pe.matmul(psv[a][:, b], one_row[:], bv_sb[:], start=False, stop=True)
                    last.then_inc(v_ready, 1)

            for p in range(2):
                pe.wait_ge(x_in[p], 16)
                chunk(p, p)
            with pe.Fori(1, NCH // 2) as cc:
                for p in range(2):
                    pe.wait_ge(x_in[p], cc * 16 + 16)
                    chunk(cc * 2 + p, p)

        @block.scalar
        def _(act):
            def high(n, b):
                if started(n):
                    act.wait_ge(rotated, n + 1)
                    act.wait_ge(parts_free[b % 2], (n - b % 2) * 8 + 16)
                    act.activation(parts[b % 2][:, 0], item[b][:], ACT.Copy).then_inc(high_done, 1)

            def middle(n, b):
                if started(n):
                    act.wait_ge(rest_done, n + 1)
                    act.activation(parts[b % 2][:, 1], item[b][:], ACT.Copy).then_inc(middle_done, 1)

            def chunk(c):
                for m in range(ITEMS):
                    ft, t = m // 2, m % 2
                    n = c * ITEMS + m
                    high(n - 2, (m - 2) % RING)
                    act.wait_ge(projected, n + 1)
                    act.wait_ge(low_done, n + 1)
                    act.activation(item[m][:], ps[m][:], ACT.Identity, bias=b_sb[:, t, ft:ft + 1]).then_inc(biased, 1)
                    middle(n - 2, (m - 2) % RING)
                    if m >= ITEMS - 2:
                        a = m - (ITEMS - 2)
                        act.wait_ge(v_ready, c * 2 + a + 1)
                        for b in range(2):
                            dst = v_all[:, :, bass.ds(c * TT + 2 * a + b, 1), :, 0:HD]
                            last = act.activation(dst.rearrange("p g a j d -> p (g a) j d"),
                                                  psv[a][:, b].rearrange("p (g j d) -> p g j d", g=NG, j=HG), ACT.Copy)
                        last.then_inc(v_free, 1)

            act.wait_ge(b_in, 32)
            chunk(0)
            chunk(1)
            with act.Fori(2, NCH) as c:
                chunk(c)
            for n in range(TOTAL - 2, TOTAL):
                high(n, n % RING)
                middle(n, n % RING)
            act.wait_ge(v_free, 2 + 2 * NCH)

        @block.vector
        def _(dve):
            def rest(n, b):
                if started(n):
                    dve.wait_ge(high_done, n + 1)
                    dve.tensor_tensor(item[b][:], item[b][:], parts[b % 2][:, 0], ALU.subtract).then_inc(rest_done, 1)

            def low(n, b):
                if started(n):
                    dve.wait_ge(middle_done, n + 1)
                    dve.tensor_tensor(parts[b % 2][:, 2], item[b][:], parts[b % 2][:, 1], ALU.subtract)\
                        .then_inc(low_done, 1)

            def chunk(c, p):
                for m in range(ITEMS):
                    n = c * ITEMS + m
                    if started(n - 2):
                        dve.wait_ge(rotated, n - 1)
                    dve.wait_ge(biased, n + 1)
                    dve.sem_inc(waited, 1)
                    dve.stream_shuffle(pair[m % 2][:], item[m][:], [q ^ 1 for q in range(32)]).then_inc(swapped, 1)
                    dve.wait_ge(swapped, n + 1)
                    dve.tensor_tensor(item[m][:], item[m][:], table[p][:, 0], ALU.mult).then_inc(cosine_done, 1)
                    rest(n - 1, (m - 1) % RING)
                    dve.wait_ge(cosine_done, n + 1)
                    dve.wait_ge(sine_done, n + 1)
                    dve.tensor_tensor(item[m][:], item[m][:], pair[m % 2][:], ALU.add).then_inc(rotated, 1)
                    low(n - 1, (m - 1) % RING)

            dve.sem_inc(low_done, RING)
            dve.sem_inc(v_free, 2)
            for b in range(2):
                dve.sem_inc(parts_free[b], 16)
            for p in range(2):
                dve.wait_ge(table_in[p], 32)
                chunk(p, p)
            with dve.Fori(1, NCH // 2) as cc:
                for p in range(2):
                    dve.wait_ge(table_in[p], cc * 32 + 32)
                    chunk(cc * 2 + p, p)
            rest(TOTAL - 1, (TOTAL - 1) % RING)
            low(TOTAL - 1, (TOTAL - 1) % RING)


def attend(nc, io, q_parts, k_parts, heads_dram, w_dram, low_bits, v_all, k_all, first_q):
    with ExitStack() as ctx:
        def sb(name, shape, dt=F32):
            return ctx.enter_context(nc.sbuf_tensor(name, shape, dt))

        def psum(name, shape):
            return ctx.enter_context(nc.psum_tensor(name, shape, F32))

        def sem(name):
            return ctx.enter_context(nc.semaphore(name))

        RING, BANKS = 8, 3
        QT = HG * TT
        WIDE = 2 * CH
        MAXG = QT * S // WIDE
        TILES = KT * HG
        UNITS = NCH * NG
        LEAD = 4
        TURN_AT = TILES - (LEAD - 1) * HG + 2
        SLOTS = TILES + 1
        ROUNDS = 4

        q_sb = [first_q] + [sb(f"q_sb{g}", [ROWS, HG, CH], BF16) for g in range(1, NG)]
        probs = [sb(f"probs{r}", [P, CH]) for r in range(RING)]
        mixed = [sb(f"mixed{p}", [P, CH]) for p in range(2)]
        ident = sb("ident", [P, P])
        group_max = sb("group_max", [P, MAXG])
        top = sb("top", [P, QT])
        shift = sb("shift", [QT, P])
        shift_rest = sb("shift_rest", [QT, P])
        shift_parts = sb("shift_parts", [QT, 3, P], BF16)
        SCAN = W_TOTAL // P // UNITS
        w_words = sb("w_words", [P, SCAN], I32)
        bits = sb("bits", [P, SCAN], I32)
        scores = [psum(f"scores{b}", [P, CH]) for b in range(BANKS)]
        wide = [psum(f"wide{b}", [P, 2, CH]) for b in range(2)]
        sums = psum("sums", [P, CH])

        k_in = sem("last_k_in")
        q_in = [sem(f"q_in{g}") for g in range(NG)]
        k_ones = sem("k_ones")
        ident_set = sem("ident_set")
        wide_ready = sem("wide_ready")
        wide_free = sem("wide_free")
        top_ready = sem("top_ready")
        first_turn = sem("first_turn")
        part_step = sem("part_step")
        waited = sem("pool_waited")
        shift_in = sem("shift_in")
        scored = sem("scored")
        exps_done = sem("exps_done")
        probs_free = sem("probs_free")
        w_copied = sem("w_copied")
        words_in = sem("words_in")
        scanned = sem("scanned")
        sums_free = sem("sums_free")
        mixed_free = [sem(f"mixed_free{p}") for p in range(2)]

        GROUPS = MAXG // KT

        def slot(n, turn=True):
            return n + 1 if turn and n >= TURN_AT else n

        block = ctx.enter_context(nc.Block())

        @block.sync
        def _(sp):
            def load_q(c, g):
                place_q(sp, q_parts, q_sb[g], c, g, q_in[g])

            def place_shift(u, g):
                sp.wait_ge(part_step, (u + 2) * ROUNDS)
                for a in range(3):
                    row = q_sb[g][SHIFT_ROW + a:SHIFT_ROW + a + 1].rearrange("o j (t s) -> o (j t) s", t=TT)
                    sp.dma_start(row, shift_parts[:, a]).then_inc(shift_in, 16)

            def finish(c, g):
                sp.wait_ge(sums_free, c * NG + g + 2)
                sp.dma_start(heads_dram[bass.ds(c, 1), :, g].rearrange("c p s -> (c p) s"), mixed[g % 2][:])\
                    .then_inc(mixed_free[g % 2], 16)

            place_k(sp, k_parts, k_all, NCH - 1, FT - 1, k_in)
            for g in range(1, NG):
                load_q(0, g)
            for name, (at, rows, cols) in W_AT.items():
                sp.dma_start(w_dram[at:at + rows * cols].rearrange("(r c) -> r c", c=cols), io[name]).then_inc(w_copied, 16)
            sp.wait_ge(w_copied, 16 * len(W_AT))

            def load_words(u):
                sp.wait_ge(scanned, u + 1)
                words = w_dram.bitcast(I32).rearrange("(u p n) -> u p n", u=UNITS, p=P)[bass.ds(u, 1)]
                sp.dma_start(w_words[:], words.rearrange("u p n -> (u p) n")).then_inc(words_in, 16)

            load_words(0)
            place_shift(0, 0)
            with sp.Fori(0, NCH - 1) as c:
                for g in range(NG):
                    load_words(c * NG + g + 1)
                    place_shift(c * NG + g + 1, (g + 1) % NG)
                    finish(c, g)
                    load_q(c + 1, g)
            for g in range(NG):
                if g < NG - 1:
                    load_words((NCH - 1) * NG + g + 1)
                    place_shift((NCH - 1) * NG + g + 1, g + 1)
                finish(NCH - 1, g)
            for p in range(2):
                sp.wait_ge(mixed_free[p], 16 + 16 * UNITS // 2)

        @block.gpsimd
        def _(pool):
            pool.memset(ident[:], 0.0).then_inc(ident_set, 1)
            pool.wait_ge(ident_set, 1)
            pool.affine_select(out=ident[:], in_=ident[:], compare_op=ALU.not_equal, fill=1.0, base=0,
                               pattern=[[-1, P]], channel_multiplier=1).then_inc(ident_set, 1)
            pool.wait_ge(ident_set, 2)
            for g in range(NG):
                pool.memset(k_all[SHIFT_ROW:ROWS, g], 1.0).then_inc(k_ones, 1)
                pool.wait_ge(k_ones, g + 1)
            pool.sem_inc(part_step, ROUNDS)

            def split_shift(u):
                base = (u + 1) * ROUNDS
                pool.wait_ge(shift_in, u * 48 + 48)
                pool.wait_ge(part_step, base)
                pool.sem_inc(waited, 1)
                pool.tensor_copy(shift_parts[:, 0], shift[:]).then_inc(part_step, 1)
                pool.wait_ge(part_step, base + 1)
                pool.tensor_tensor(shift_rest[:], shift[:], shift_parts[:, 0], ALU.subtract).then_inc(part_step, 1)
                pool.wait_ge(part_step, base + 2)
                pool.sem_inc(waited, 1)
                pool.tensor_copy(shift_parts[:, 1], shift_rest[:]).then_inc(part_step, 1)
                pool.wait_ge(part_step, base + 3)
                pool.tensor_tensor(shift_parts[:, 2], shift_rest[:], shift_parts[:, 1], ALU.subtract)\
                    .then_inc(part_step, 1)

            pool.wait_ge(exps_done, BANKS)
            split_shift(0)
            with pool.Fori(1, UNITS) as u:
                pool.wait_ge(exps_done, (u - 1) * SLOTS + TURN_AT + 1 + BANKS)
                split_shift(u)

        @block.tensor
        def _(pe):
            def max_group(c, g, n):
                if n == 0:
                    max_start(c, g)
                u = c * NG + g
                j, t, b = n // (TT * 4), n // 4 % TT, n % 4
                pe.wait_ge(wide_free, u * MAXG + n + 1)
                for h in range(2):
                    keys = slice((2 * b + h) * CH, (2 * b + h + 1) * CH)
                    last = pe.matmul(wide[n % 2][:, h], q_sb[g][0:SHIFT_ROW, j, t * P:(t + 1) * P],
                                     k_all[0:SHIFT_ROW, g, j, keys], start=True, stop=True)
                last.then_inc(wide_ready, 1)

            def max_turn(u, bank, done):
                pe.wait_ge(top_ready, u + 1)
                pe.transpose(scores[bank][0:QT, 0:P], top[:], ident[:]).then_inc(done, 1)

            def max_start(c, g):
                if not isinstance(c, int) or g >= NG // FT:
                    pe.wait_ge(k_in, 16 * NPROD)
                if g > 0:
                    pe.wait_ge(q_in[g], c * (16 * NPROD) + 16 * NPROD)
                elif not (isinstance(c, int) and c == 0):
                    pe.wait_ge(q_in[g], c * (16 * NPROD))

            def sum_over(u, g, kt, turn=True):
                if kt == 0:
                    pe.wait_ge(sums_free, u + 1)
                pe.wait_ge(exps_done, u * SLOTS + slot(kt * HG + HG - 1, turn) + 1 + BANKS)
                for j in range(HG):
                    last = pe.matmul(sums[32 * j:32 * j + HD + 1, :], v_all[:, g, kt, j], probs[(kt * HG + j) % RING][:],
                                     start=(kt == 0), stop=(kt == KT - 1))
                last.then_inc(probs_free, 1)

            def after(c, g):
                return c + (g + 1) // NG, (g + 1) % NG

            def groups_beside(c, g, kt, left):
                steps = 1 + (kt + LEAD) // KT
                if steps > left:
                    return []
                for _ in range(steps):
                    c, g = after(c, g)
                kt = (kt + LEAD) % KT
                return [(c, g, n) for n in range(kt * GROUPS, (kt + 1) * GROUPS)]

            def unit(c, g, first=False, left=2):
                u = c * NG + g
                pe.wait_ge(shift_in, u * 48 + 96)
                for kt in range(KT):
                    groups = groups_beside(c, g, kt, left)
                    for j in range(HG):
                        n = kt * HG + j
                        if j % (HG - 1) == 0 and groups:
                            max_group(*groups[j // (HG - 1)])
                        if n == TURN_AT and left > 0:
                            pe.wait_ge(exps_done, u * SLOTS + n + 1)
                            max_turn(u + 1, n % BANKS, scored)
                        s = slot(n, left > 0)
                        pe.wait_ge(exps_done, u * SLOTS + s + 1)
                        pe.matmul(scores[s % BANKS][:], k_all[:, g, j, kt * P:(kt + 1) * P], q_sb[g][:, j],
                                  start=True, stop=True).then_inc(scored, 1)
                    if kt > 0:
                        sum_over(u, g, kt - 1, left > 0)
                    elif not first:
                        sum_over(u - 1, (g - 1) % NG, KT - 1)

            pe.wait_ge(ident_set, 2)
            for n in range(MAXG):
                max_group(0, 0, n)
            for n in range(LEAD * GROUPS):
                max_group(0, 1, n)
                if n == 1:
                    max_turn(0, 0, first_turn)
            pe.wait_ge(k_ones, NG)
            unit(0, 0, first=True)
            with pe.Fori(0, NCH - 1) as c:
                for g in range(1, NG):
                    unit(c, g)
                unit(c + 1, 0)
            for g in range(1, NG):
                unit(NCH - 1, g, left=min(2, NG - 1 - g))
            sum_over(UNITS - 1, NG - 1, KT - 1, False)

        @block.scalar
        def _(act):
            act.sem_inc(probs_free, RING // HG)
            act.wait_ge(first_turn, 1)
            act.activation(shift[:], scores[0][0:QT, 0:P], ACT.Copy, scale=-1.0).then_inc(exps_done, BANKS)

            def take_sums(c, g):
                act.wait_ge(probs_free, (c * NG + g + 1) * KT + RING // HG)
                act.wait_ge(mixed_free[g % 2], (c * 2 + g // 2) * 16 + 16)
                act.activation(mixed[g % 2][:], sums[:], ACT.Copy).then_inc(sums_free, 1)

            def unit(c, g, first=False, last=False):
                u = c * NG + g
                for n in range(TILES):
                    if n == TURN_AT and not last:
                        act.wait_ge(scored, u * SLOTS + n + 1)
                        act.wait_ge(part_step, (u + 2) * ROUNDS)
                        act.activation(shift[:], scores[n % BANKS][0:QT, 0:P], ACT.Copy, scale=-1.0)\
                            .then_inc(exps_done, 1)
                    s = slot(n, not last)
                    if n % HG == 0:
                        act.wait_ge(probs_free, u * KT + n // HG + 1)
                    act.wait_ge(scored, u * SLOTS + s + 1)
                    act.activation(probs[n % RING][:], scores[s % BANKS][:], ACT.Exp, scale=INV_SCALE)\
                        .then_inc(exps_done, 1)
                    if n == HG - 1 and not first:
                        take_sums(*((c, g - 1) if g > 0 else (c - 1, NG - 1)))

            unit(0, 0, first=True)
            with act.Fori(0, NCH - 1) as c:
                for g in range(1, NG):
                    unit(c, g)
                unit(c + 1, 0)
            for g in range(1, NG):
                unit(NCH - 1, g, last=g == NG - 1)
            take_sums(NCH - 1, NG - 1)

        @block.vector
        def _(dve):
            def maxima(u):
                if not (isinstance(u, int) and u == 0):
                    dve.wait_ge(top_ready, u)
                for n in range(MAXG):
                    dve.wait_ge(wide_ready, u * MAXG + n + 1)
                    dve.reduce_max(group_max[:, n:n + 1], wide[n % 2][:], mybir.AxisListType.XY).then_inc(wide_free, 1)
                dve.wait_ge(wide_free, (u + 1) * MAXG + 2)
                if isinstance(u, int):
                    if u == 1:
                        dve.wait_ge(first_turn, 1)
                else:
                    dve.wait_ge(scored, (u - 2) * SLOTS + TURN_AT + 1)
                dve.reduce_max(top[:], group_max[:].rearrange("q (r b) -> q r b", b=4), AX_X).then_inc(top_ready, 1)

            for p in range(2):
                dve.sem_inc(mixed_free[p], 16)
            dve.sem_inc(wide_free, 2)
            dve.sem_inc(shift_in, 48)

            def scan(u):
                dve.wait_ge(words_in, u * 16 + 16)
                dve.wait_ge(scanned, u + 1)
                dve.scalar_tensor_tensor(out=bits[:], in0=w_words[:], scalar=LOW_BITS, in1=bits[:],
                                         op0=ALU.bitwise_and, op1=ALU.bitwise_or).then_inc(scanned, 1)

            dve.memset(bits[:], 0).then_inc(scanned, 1)
            maxima(0)
            dve.memset(sums[:], 0.0).then_inc(sums_free, 1)
            scan(0)
            maxima(1)
            scan(1)
            with dve.Fori(2, UNITS) as u:
                maxima(u)
                scan(u)
            dve.wait_ge(scanned, UNITS + 1)
            dve.reduce_max(low_bits[:], bits[:], AX_X).then_inc(scanned, 1)
            dve.wait_ge(scanned, UNITS + 2)


def feed_forward(nc, io, heads_dram, shares_dram, w_dram, low_bits, out):
    with ExitStack() as ctx:
        def sb(name, shape, dt=F32):
            return ctx.enter_context(nc.sbuf_tensor(name, shape, dt))

        def psum(name, shape):
            return ctx.enter_context(nc.psum_tensor(name, shape, F32))

        def sem(name):
            return ctx.enter_context(nc.semaphore(name))

        wo = sb("wo", [P, NG, D])
        w_sb = {name: sb(name, [P, rows // P, cols]) for name, (_, rows, cols) in W_AT.items()}
        scale = sb("scale", [P, 4, HT])
        scale3 = sb("scale3", [P, D])
        ident = sb("ident_ff", [P, P])
        ones = sb("ones", [P, 1])
        flag = sb("flag", [1, 1], I32)
        heads = sb("heads_sb", [P, NG, CH])
        inverse_sums = sb("inverse_sums", [P, HG * NG * CH // P])
        shares = [sb(f"shares{b}", [P, CH]) for b in range(2)]
        x_sb = sb("x_sb", [P, TT, D])
        x1 = [sb(f"x1_{p}", [P, TT, D]) for p in range(2)]
        x1t = [sb(f"x1t_{h}", [P, FT, CH], F32R) for h in range(2)]
        hid_a = [sb(f"hid_a{h}", [P, HT, CH], F32R) for h in range(2)]
        hid_b = [sb(f"hid_b{h}", [P, HT, CH], F32R) for h in range(2)]
        gate = [sb(f"gate{b}", [P, CH]) for b in range(2)]
        whole = [sb(f"whole_hid{b}", [P, CH]) for b in range(4)]
        fin = sb("fin", [P, TT, D])
        stats = [sb(f"stats{i}", [P, TT, 6]) for i in range(2)]
        moments = [sb(f"moments{i}", [P, TT, 2]) for i in range(2)]
        spread = [sb(f"spread{i}", [P, TT]) for i in range(2)]
        root = [sb(f"root{i}", [P, TT]) for i in range(2)]
        inverse = [sb(f"inverse{i}", [P, TT]) for i in range(2)]
        acc = [psum(f"acc{b}", [P, CH]) for b in range(4)]
        tok = [psum(f"tok{b}", [P, 2, D]) for b in range(2)]
        flip = [psum(f"flip{b}", [P, CH]) for b in range(2)]

        small_in = sem("small_in")
        w_in = {name: sem(f"{name}_in") for name in W_AT}
        heads_in = sem("heads_in")
        x_in = sem("x_ff_in")
        wo_zero = sem("wo_zero")
        ident_set = sem("ident_ff_set")
        bits_summed = sem("bits_summed")
        flag_set = sem("flag_set")
        acc_ready = sem("acc_ready")
        gated = sem("gated")
        product = sem("product")
        gelu_done = sem("gelu_done")
        rounded = sem("rounded")
        hid_ready = sem("hid_ready")
        tok_ready = sem("tok_ready")
        first_sums_in, sums_in = sem("first_sums_in"), sem("sums_in")
        inverted = sem("inverted")
        first_inverse_out, inverse_out = sem("first_inverse_out"), sem("inverse_out")
        first_shares_in = [sem(f"first_shares_in{b}") for b in range(2)]
        shares_in = [sem(f"shares_in{b}") for b in range(2)]
        divided = sem("divided")
        pool_waited = sem("pool_ff_waited")
        norm1 = sem("norm1")
        norm2 = sem("norm2")
        root_done = sem("root_done")
        flip_ready = sem("flip_ready")
        x1t_step = sem("x1t_step")
        waited = sem("ff_waited")
        fin_free = sem("fin_free")

        ACCS = 4 * HT
        HIDS = 3 * HT
        SUM_COLS = HG * NG * CH // P
        SUM_ROWS = P // HG
        NORM1 = 4 * TT + 2
        NORM2 = 5 * TT + 2
        SMALL = HG + 4 + 1
        EARLY = 3

        block = ctx.enter_context(nc.Block())

        def load_sums(engine, c, done):
            for j in range(HG):
                src = heads_dram[bass.ds(c, 1), 32 * j + HD].rearrange("c g (a b) -> (c g a) b", b=SUM_COLS)
                engine.dma_start(inverse_sums[j * SUM_ROWS:(j + 1) * SUM_ROWS], src).then_inc(done, 16)

        def store_inverse(engine, c, done):
            dst = shares_dram[bass.ds(c, 1)].rearrange("c j g (a b) -> (c j g a) b", b=SUM_COLS)
            engine.dma_start(dst, inverse_sums[:]).then_inc(done, 16)

        def load_shares(engine, c, g, done):
            for j in range(HG):
                src = shares_dram[bass.ds(c, 1), j, g].rearrange("c s -> (c s)").partition_broadcast(32)
                engine.dma_start(shares[g % 2][32 * j:32 * j + 32], src).then_inc(done[g % 2], 16)

        @block.sync
        def _(sp):
            def load_heads(c):
                sp.dma_start(heads[:], heads_dram[bass.ds(c, 1)].rearrange("c p g s -> (c p) g s")).then_inc(heads_in, 16)
                sp.dma_start(x_sb[:], io["x"].rearrange("(c t p) d -> c p t d", t=TT, p=P)[bass.ds(c, 1)]
                             .rearrange("c p t d -> (c p) t d")).then_inc(x_in, 16)

            def store(c):
                sp.wait_ge(norm2, (c + 2) * NORM2)
                sp.dma_start(out.rearrange("(c t p) d -> c p t d", t=TT, p=P)[bass.ds(c, 1)]
                             .rearrange("c p t d -> (c p) t d"), fin[:]).then_inc(fin_free, 16)

            load_sums(sp, 0, first_sums_in)
            load_heads(0)
            sp.wait_ge(inverted, 1)
            store_inverse(sp, 0, first_inverse_out)
            sp.wait_ge(wo_zero, 1)
            for j in range(HG):
                sp.dma_start(wo[32 * j:32 * j + HD], io["woT"].rearrange("(g j d) o -> j d g o", g=NG, j=HG)[j])\
                    .then_inc(small_in, 16)
            for n, name in enumerate(["w1_s", "w2_s", "h1_s", "h2_s"]):
                sp.dma_start(scale[:, n], io[name]).then_inc(small_in, 16)
            sp.dma_start(scale3[:], io["w3_s"].partition_broadcast(P)).then_inc(small_in, 16)
            sp.wait_ge(first_inverse_out, 16)
            for g in range(NG):
                if g >= 2:
                    sp.wait_ge(divided, g - 1)
                load_shares(sp, 0, g, first_shares_in)
            for name, (at, rows, cols) in W_AT.items():
                src = w_dram[at:at + rows * cols].rearrange("(t p o) -> p t o", p=P, o=cols)
                sp.dma_start(w_sb[name][:], src).then_inc(w_in[name], 16)
            sp.wait_ge(norm1, NORM1)
            load_heads(1)
            with sp.Fori(0, NCH - 2) as c:
                sp.wait_ge(norm1, (c + 2) * NORM1)
                load_heads(c + 2)
                store(c)
            for c in range(NCH - 2, NCH):
                store(c)
            sp.wait_ge(fin_free, 16 + 16 * NCH)

        @block.gpsimd
        def _(pool):
            pool.memset(wo[:], 0.0).then_inc(wo_zero, 1)
            pool.wait_ge(wo_zero, 1)
            pool.memset(ones[:], 1.0).then_inc(ident_set, 1)
            pool.wait_ge(ident_set, 1)
            pool.memset(ident[:], 0.0).then_inc(ident_set, 1)
            pool.wait_ge(ident_set, 2)
            pool.affine_select(out=ident[:], in_=ident[:], compare_op=ALU.not_equal, fill=1.0, base=0,
                               pattern=[[-1, P]], channel_multiplier=1).then_inc(ident_set, 1)

            pool.wait_ge(first_inverse_out, 16)
            with pool.Fori(1, NCH) as c:
                load_sums(pool, c, sums_in)
                pool.wait_ge(inverted, c + 1)
                pool.sem_inc(pool_waited, 1)
                store_inverse(pool, c, inverse_out)
                for g in range(NG):
                    pool.wait_ge(divided, c * NG + g - 1)
                    if g == 0:
                        pool.wait_ge(inverse_out, c * 16)
                    pool.sem_inc(pool_waited, 1)
                    load_shares(pool, c, g, shares_in)

        def front_turn(c):
            return 0 if isinstance(c, int) and c == 0 else c * 2 - 1

        def back_turn(c, last):
            return c * 2 + 1 if last else c * 2 + 2

        @block.tensor
        def _(pe):
            def front(c):
                pe.wait_ge(divided, c * NG + NG)
                for t in range(TT):
                    if t % 2 == 0 and not (isinstance(c, int) and c == 0):
                        pe.wait_ge(norm2, (c - 1) * NORM2 + t + 2)
                    for g in range(NG):
                        last = pe.matmul(tok[t // 2][:, t % 2], heads[:, g, t * P:(t + 1) * P], wo[:, g],
                                         start=(g == 0), stop=(g == NG - 1))
                    if t % 2 == 1:
                        last.then_inc(tok_ready, 1)

            def front_flip(c, p):
                pe.wait_ge(norm1, c * NORM1 + NORM1)
                for f in range(FT):
                    for t in range(TT):
                        last = pe.transpose(flip[f][:, t * P:(t + 1) * P], x1[p][:, t, f * P:(f + 1) * P], ident[:])
                    last.then_inc(flip_ready, 1)

            def acc_read(c, n):
                if n < 2 * HT and n % 2 == 0:
                    pe.wait_ge(gated, c * HT + n // 2 + 1)
                elif n < 2 * HT:
                    pe.wait_ge(product, c * HT + n // 2 + 1)
                else:
                    pe.wait_ge(gelu_done, c * 2 * HT + n - 2 * HT + 1)

            def net(view):
                def term(dst, w, src, i, first, last):
                    for h in range(2):
                        mm = pe.matmul(dst, w.bitcast(view), src[h].bitcast(view),
                                       start=(first and h == 0), stop=(last and h == 1))
                    return mm

                def gate_layer(c):
                    pe.wait_ge(x1t_step, c * 2 * FT + 2 * FT)
                    for o in range(HT):
                        for w, name in enumerate(("w1T", "w2T")):
                            n = 2 * o + w
                            if n >= 4:
                                acc_read(c, n - 4)
                            for i in range(FT):
                                mm = term(acc[n % 4][:], w_sb[name][:, i, o * P:(o + 1) * P],
                                          [x[:, i] for x in x1t], i, i == 0, i == FT - 1)
                            mm.then_inc(acc_ready, 1)

                def hidden_layer(c, layer):
                    src, wt = ((hid_a, w_sb["h1T"]), (hid_b, w_sb["h2T"]))[layer]

                    def some(o, tiles):
                        for i in tiles:
                            if o == 0:
                                pe.wait_ge(hid_ready, c * HIDS + layer * HT + i + 1)
                            mm = term(acc[o % 4][:], wt[:, i, o * P:(o + 1) * P], [x[:, i] for x in src],
                                      i, i == 0, i == HT - 1)
                        return mm

                    for o in range(EARLY):
                        acc_read(c, (2 + layer) * HT + o - 4)
                        some(o, range(HT - 1))
                    for o in range(EARLY):
                        some(o, [HT - 1]).then_inc(acc_ready, 1)
                    for o in range(EARLY, HT):
                        acc_read(c, (2 + layer) * HT + o - 4)
                        some(o, range(HT)).then_inc(acc_ready, 1)

                def back(c, final):
                    def some(t, tiles):
                        for i in tiles:
                            for h in range(2):
                                mm = pe.matmul(tok[t // 2][:, t % 2], hid_a[h][:, i, t * P:(t + 1) * P].bitcast(view),
                                               w_sb["w3T"][:, i].bitcast(view),
                                               start=(i == 0 and h == 0), stop=(i == HT - 1 and h == 1))
                        return mm

                    pe.wait_ge(hid_ready, c * HIDS + HIDS - 1)
                    for t in (0, 2):
                        if final:
                            pe.wait_ge(norm2, c * NORM2 + t + 2)
                        some(t, range(HT - 1))
                    pe.wait_ge(hid_ready, c * HIDS + HIDS)
                    for t in (0, 2):
                        some(t, [HT - 1])
                    for t in (1, 3):
                        some(t, range(HT)).then_inc(tok_ready, 1)

                def step(c, p, final=False):
                    hidden_layer(c, 0)
                    if not final:
                        front(c + 1)
                    hidden_layer(c, 1)
                    if not final:
                        front_flip(c + 1, 1 - p)
                    back(c, final)
                    if not final:
                        gate_layer(c + 1)

                for name in ("w1T", "w2T"):
                    pe.wait_ge(w_in[name], 16)
                gate_layer(0)
                for name in ("h1T", "h2T", "w3T"):
                    pe.wait_ge(w_in[name], 16)
                with pe.Fori(0, NCH // 2 - 1) as half:
                    for p in range(2):
                        step(half * 2 + p, p)
                step(NCH - 2, 0)
                step(NCH - 1, 1, final=True)

            pe.wait_ge(ident_set, 3)
            pe.matmul(flip[0][0:1, 0:1], low_bits[:], ones[:], start=True, stop=True).then_inc(bits_summed, 1)
            pe.wait_ge(small_in, 16 * SMALL)
            front(0)
            pe.wait_ge(flag_set, 1)
            front_flip(0, 0)
            low = pe.value_load(flag[0:1, 0:1], min_val=0, max_val=1)
            with pe.If(low < 1):
                net(F32R)
            with pe.Else():
                net(F32)

        @block.scalar
        def _(act):
            def front_root(c):
                act.wait_ge(norm1, c * NORM1 + 3 * TT + 1)
                act.activation(root[0][:], spread[0][:], ACT.Sqrt).then_inc(root_done, 1)

            def gates(c):
                for o in range(HT):
                    if o >= 2:
                        act.wait_ge(product, c * HT + o - 1)
                    act.wait_ge(acc_ready, c * ACCS + 2 * o + 1)
                    act.activation(gate[o % 2][:], acc[(2 * o) % 4][:], ACT.Silu, scale=scale[:, 0, o:o + 1])\
                        .then_inc(gated, 1)

            def gelus(c, layer, tiles):
                for o in tiles:
                    n = (2 + layer) * HT + o
                    act.wait_ge(hid_ready, c * HIDS + (1 + layer) * HT + o - 3)
                    act.wait_ge(acc_ready, c * ACCS + n + 1)
                    act.activation(whole[o % 4][:], acc[n % 4][:], ACT.Gelu, scale=scale[:, 2 + layer, o:o + 1])\
                        .then_inc(gelu_done, 1)

            def back_root(c):
                act.wait_ge(norm2, (c + 1) * NORM2 + 4 * TT + 1)
                act.activation(root[1][:], spread[1][:], ACT.Sqrt).then_inc(root_done, 1)

            def step(c, p, final=False):
                gelus(c, 0, range(HT))
                gelus(c, 1, range(3))
                if not final:
                    front_root(c + 1)
                gelus(c, 1, range(3, HT))
                if not final:
                    gates(c + 1)
                back_root(c)

            act.wait_ge(small_in, 16 * SMALL)
            front_root(0)
            gates(0)
            with act.Fori(0, NCH // 2 - 1) as half:
                for p in range(2):
                    step(half * 2 + p, p)
            step(NCH - 2, 0)
            step(NCH - 1, 1, final=True)

        @block.vector
        def _(dve):
            def stats_of(i, data, done, base):
                for t in range(TT):
                    dve.wait_ge(done, base - TT + t + 1)
                    dve.bn_stats(stats[i][:, t], data[:, t]).then_inc(done, 1)
                for t in range(TT):
                    dve.wait_ge(done, base + t + 1)
                    dve.sem_inc(waited, 1)
                    dve.bn_aggr(moments[i][:, t], stats[i][:, t]).then_inc(done, 1)
                dve.wait_ge(done, base + 2 * TT)
                dve.tensor_scalar(spread[i][:], moments[i][:, :, 1], EPS, None, ALU.add).then_inc(done, 1)

            def apply(i, data, done, base, turn):
                dve.wait_ge(root_done, turn + 1)
                dve.reciprocal(inverse[i][:], root[i][:]).then_inc(done, 1)
                dve.wait_ge(done, base + 2 * TT + 2)
                for t in range(TT):
                    dve.tensor_scalar(data[:, t], data[:, t], moments[i][:, t, 0:1], inverse[i][:, t:t + 1],
                                      ALU.subtract, ALU.mult).then_inc(done, 1)

            def invert(c):
                if isinstance(c, int) and c == 0:
                    dve.wait_ge(first_sums_in, HG * 16)
                else:
                    dve.wait_ge(sums_in, c * HG * 16)
                dve.reciprocal(inverse_sums[:], inverse_sums[:]).then_inc(inverted, 1)

            def divide(c, g):
                if g == 0:
                    dve.wait_ge(heads_in, c * 16 + 16)
                if isinstance(c, int) and c == 0:
                    dve.wait_ge(first_shares_in[g % 2], (g // 2 + 1) * HG * 16)
                else:
                    dve.wait_ge(shares_in[g % 2], ((c - 1) * 2 + g // 2 + 1) * HG * 16)
                dve.tensor_tensor(heads[:, g], heads[:, g], shares[g % 2][:], ALU.mult).then_inc(divided, 1)

            def front_stats(c, p):
                dve.wait_ge(x_in, c * 16 + 16)
                for t in range(TT):
                    if t % 2 == 0:
                        dve.wait_ge(tok_ready, front_turn(c) * 2 + t // 2 + 1)
                    dve.tensor_tensor(x1[p][:, t], tok[t // 2][:, t % 2], x_sb[:, t], ALU.add).then_inc(norm1, 1)
                stats_of(0, x1[p], norm1, c * NORM1 + TT)

            def front_apply(c, p):
                apply(0, x1[p], norm1, c * NORM1 + TT, front_turn(c))

            def front_split(c):
                for f in range(FT):
                    dve.wait_ge(flip_ready, c * FT + f + 1)
                    dve.tensor_copy(x1t[0][:, f], flip[f][:]).then_inc(x1t_step, 1)
                    dve.wait_ge(x1t_step, c * 2 * FT + 2 * f + 1)
                    dve.tensor_tensor(x1t[1][:, f], flip[f][:], x1t[0][:, f].bitcast(F32), ALU.subtract)\
                        .then_inc(x1t_step, 1)

            def split(c, k):
                dst = (hid_a, hid_b, hid_a)[k // HT]
                dve.tensor_copy(dst[0][:, k % HT], whole[k % 4][:]).then_inc(rounded, 1)
                dve.wait_ge(rounded, c * HIDS + k + 1)
                dve.tensor_tensor(dst[1][:, k % HT], whole[k % 4][:], dst[0][:, k % HT].bitcast(F32), ALU.subtract)\
                    .then_inc(hid_ready, 1)

            def gates(c):
                for o in range(HT):
                    dve.wait_ge(acc_ready, c * ACCS + 2 * o + 2)
                    dve.wait_ge(gated, c * HT + o + 1)
                    dve.scalar_tensor_tensor(out=whole[o % 4][:], in0=acc[(2 * o + 1) % 4][:],
                                             scalar=scale[:, 1, o:o + 1], in1=gate[o % 2][:],
                                             op0=ALU.mult, op1=ALU.mult).then_inc(product, 1)
                    dve.wait_ge(product, c * HT + o + 1)
                    split(c, o)

            def gelu_split(c, layer, o):
                dve.wait_ge(gelu_done, (c * 2 + layer) * HT + o + 1)
                split(c, (1 + layer) * HT + o)

            def back(c, p, final):
                turn, base = back_turn(c, final), (c + 1) * NORM2
                dve.wait_ge(fin_free, c * 16 + 16)
                for t in range(TT):
                    if t % 2 == 0:
                        dve.wait_ge(tok_ready, turn * 2 + t // 2 + 1)
                    dve.tensor_tensor(fin[:, t], tok[t // 2][:, t % 2], scale3[:], ALU.mult).then_inc(norm2, 1)
                for t in range(TT):
                    dve.wait_ge(norm2, base + t + 1)
                    dve.tensor_tensor(fin[:, t], fin[:, t], x1[p][:, t], ALU.add).then_inc(norm2, 1)
                stats_of(1, fin, norm2, base + 2 * TT)
                apply(1, fin, norm2, base + 2 * TT, turn)

            def step(c, p, more=True, final=False):
                if not final:
                    for g in range(2):
                        divide(c + 1, g)
                for o in range(HT):
                    gelu_split(c, 0, o)
                    if not final and o < 2:
                        divide(c + 1, 2 + o)
                gelu_split(c, 1, 0)
                if not final:
                    front_stats(c + 1, 1 - p)
                gelu_split(c, 1, 1)
                gelu_split(c, 1, 2)
                if not final:
                    front_apply(c + 1, 1 - p)
                for o in range(3, HT):
                    gelu_split(c, 1, o)
                if not final:
                    front_split(c + 1)
                    gates(c + 1)
                if more:
                    invert(c + 2)
                back(c, p, final)

            dve.sem_inc(norm2, NORM2)
            dve.sem_inc(fin_free, 16)
            dve.wait_ge(bits_summed, 1)
            dve.tensor_scalar(flag[:], flip[0][0:1, 0:1], 1.0, None, ALU.min).then_inc(flag_set, 1)
            invert(0)
            for g in range(NG):
                divide(0, g)
            dve.wait_ge(small_in, 16 * SMALL)
            front_stats(0, 0)
            front_apply(0, 0)
            front_split(0)
            gates(0)
            invert(1)
            with dve.Fori(0, NCH // 2 - 1) as half:
                for p in range(2):
                    step(half * 2 + p, p)
            step(NCH - 2, 0, more=False)
            step(NCH - 1, 1, more=False, final=True)


def build(nc, io, out):
    parts_dram = [nc.dram_tensor(f"{t}_parts", [3, D, S], BF16, kind="Internal").ap() for t in "qk"]
    heads_dram = nc.dram_tensor("heads", [NCH, P, NG, CH], F32, kind="Internal").ap()
    shares_dram = nc.dram_tensor("shares_dram", [NCH, HG, NG, CH], F32, kind="Internal").ap()
    w_dram = nc.dram_tensor("ff_weights", [W_TOTAL], F32, kind="Internal").ap()
    with nc.sbuf_tensor("low_bits", [P, 1], F32) as low_bits:
        with nc.sbuf_tensor("v_all", [P, NG, KT, HG, HD + 1], F32) as v_all:
            with nc.sbuf_tensor("k_all", [ROWS, NG, HG, S], BF16) as k_all, \
                    nc.sbuf_tensor("q_sb0", [ROWS, HG, CH], BF16) as first_q:
                project(nc, io, parts_dram, v_all, k_all, first_q)
                attend(nc, io, *parts_dram, heads_dram, w_dram, low_bits, v_all, k_all, first_q)
        feed_forward(nc, io, heads_dram, shares_dram, w_dram, low_bits, out)


def kernel(**inputs):
    import numpy as np
    import concourse.bacc as bacc
    from concourse.bass_utils import run_bass_kernel_spmd

    a = {k.removeprefix("L0_"): np.asarray(v) for k, v in inputs.items()}
    def columns(v):
        return v.reshape(-1, P).T

    freqs = np.float32(10000.0) ** (-np.arange(0, HD, 2).astype(np.float32) / np.float32(HD))
    angle = np.arange(S, dtype=np.float32)[:, None] * freqs[None, :]
    cos, sin = np.cos(angle), np.sin(angle)
    cos_rows = np.stack([cos, cos], axis=-1).reshape(S, HD).T
    sin_rows = np.stack([-sin, sin], axis=-1).reshape(S, HD).T

    arrays = {
        "x": a["attn_x"][0], "xT": a["attn_x"][0].T,
        "wqT": a["attn_Wq"].T, "wkT": a["attn_Wk"].T,
        "wvT": a["attn_Wv"].T, "woT": a["attn_Wo"].T,
        "bq": columns(a["attn_bq"]), "bk": columns(a["attn_bk"]), "bv": a["attn_bv"],
        "cos": np.tile(cos_rows, (P // HD, 1)), "sin": np.tile(sin_rows, (P // HD, 1)),
        "w1T": a["ffn_w1_w"].T, "w2T": a["ffn_w2_w"].T, "h1T": a["ffn_h1_w"].T, "h2T": a["ffn_h2_w"].T,
        "w3T": a["ffn_w3_w"].T,
        "w1_s": columns(a["ffn_w1_s"]), "w2_s": columns(a["ffn_w2_s"]),
        "h1_s": columns(a["ffn_h1_s"]), "h2_s": columns(a["ffn_h2_s"]), "w3_s": a["ffn_w3_s"],
    }
    arrays = {k: np.ascontiguousarray(v) for k, v in arrays.items()}
    nc = bacc.Bacc("TRN2", target_bir_lowering=False, num_devices=1)
    io = {k: nc.dram_tensor(f"in_{k}", v.shape, mybir.dt.from_np(v.dtype), kind="ExternalInput").ap()
          for k, v in arrays.items()}
    out = nc.dram_tensor("out_0", [S, D], F32, kind="ExternalOutput").ap()
    build(nc, io, out)
    r = run_bass_kernel_spmd(nc, [{f"in_{k}": v for k, v in arrays.items()}], core_ids=[0])
    return r.results[0]["out_0"].reshape(1, S, D)
```
